# Optimizing a Trainium2 kernel written in Bass

```python
import numpy as np
import jax
import jax.numpy as jnp

def _softmax(x, axis=-1):
    return jax.nn.softmax(x, axis=axis)

def _gelu(x):
    return jax.nn.gelu(x, approximate=True)

def _silu(x):
    return jax.nn.silu(x)

def _sigmoid(x):
    return jax.nn.sigmoid(x)

def _layernorm(x, axis=-1, eps=1e-05):
    m = jnp.mean(x, axis=axis, keepdims=True)
    v = jnp.var(x, axis=axis, keepdims=True)
    return (x - m) / jnp.sqrt(v + eps)

def _scatter_add(tgt, idx, src, axis=0):
    return tgt.at[idx].add(src)

def _segment_sum(src, seg, n):
    return jax.ops.segment_sum(src, seg, n)
kernel_name = 'mk_rec_standalone_d1_rec_r8_b64bfb'

def setup_inputs(seed: int=0):
    np.random.seed(seed)
    _w = jnp.asarray

    def _rec_inputs():
        import jax
        import jax.numpy as jnp
        _rk = jax.random.key(seed)
        r_item_emb_d128 = 0.000227908 + 0.99994 * jax.random.normal(jax.random.fold_in(_rk, 1), (2048, 128), jnp.float32)
        r_item_id = jax.random.randint(jax.random.fold_in(_rk, 2), (2048,), 4, 91707, jnp.int32)
        r_likes_level = jax.random.randint(jax.random.fold_in(_rk, 3), (2048,), 0, 11, jnp.int32)
        r_views_level = jax.random.randint(jax.random.fold_in(_rk, 4), (2048,), 0, 11, jnp.int32)
        r_item_seq = jnp.stack([jax.random.randint(jax.random.fold_in(jax.random.fold_in(_rk, 5), 0), (2048,), 19, 91699, jnp.int32), jax.random.randint(jax.random.fold_in(jax.random.fold_in(_rk, 5), 1), (2048,), 14, 91713, jnp.int32), jax.random.randint(jax.random.fold_in(jax.random.fold_in(_rk, 5), 2), (2048,), 0, 11464, jnp.int32), jax.random.randint(jax.random.fold_in(jax.random.fold_in(_rk, 5), 3), (2048,), 19, 91717, jnp.int32), jax.random.randint(jax.random.fold_in(jax.random.fold_in(_rk, 5), 4), (2048,), 4, 91711, jnp.int32), jax.random.randint(jax.random.fold_in(jax.random.fold_in(_rk, 5), 5), (2048,), 24, 91677, jnp.int32), jax.random.randint(jax.random.fold_in(jax.random.fold_in(_rk, 5), 6), (2048,), 14, 91711, jnp.int32), jax.random.randint(jax.random.fold_in(jax.random.fold_in(_rk, 5), 7), (2048,), 2, 91700, jnp.int32), jax.random.randint(jax.random.fold_in(jax.random.fold_in(_rk, 5), 8), (2048,), 2, 91718, jnp.int32), jax.random.randint(jax.random.fold_in(jax.random.fold_in(_rk, 5), 9), (2048,), 9, 91715, jnp.int32), jax.random.randint(jax.random.fold_in(jax.random.fold_in(_rk, 5), 10), (2048,), 7, 91714, jnp.int32), jax.random.randint(jax.random.fold_in(jax.random.fold_in(_rk, 5), 11), (2048,), 0, 91711, jnp.int32), jax.random.randint(jax.random.fold_in(jax.random.fold_in(_rk, 5), 12), (2048,), 8, 91718, jnp.int32), jax.random.randint(jax.random.fold_in(jax.random.fold_in(_rk, 5), 13), (2048,), 3, 91703, jnp.int32), jax.random.randint(jax.random.fold_in(jax.random.fold_in(_rk, 5), 14), (2048,), 2, 91710, jnp.int32), jax.random.randint(jax.random.fold_in(jax.random.fold_in(_rk, 5), 15), (2048,), 17, 91711, jnp.int32), jax.random.randint(jax.random.fold_in(jax.random.fold_in(_rk, 5), 16), (2048,), 8, 91717, jnp.int32), jax.random.randint(jax.random.fold_in(jax.random.fold_in(_rk, 5), 17), (2048,), 10, 91717, jnp.int32), jax.random.randint(jax.random.fold_in(jax.random.fold_in(_rk, 5), 18), (2048,), 3, 91706, jnp.int32), jax.random.randint(jax.random.fold_in(jax.random.fold_in(_rk, 5), 19), (2048,), 2, 91718, jnp.int32), jax.random.randint(jax.random.fold_in(jax.random.fold_in(_rk, 5), 20), (2048,), 0, 91669, jnp.int32), jax.random.randint(jax.random.fold_in(jax.random.fold_in(_rk, 5), 21), (2048,), 4, 91707, jnp.int32), jax.random.randint(jax.random.fold_in(jax.random.fold_in(_rk, 5), 22), (2048,), 9, 91703, jnp.int32), jax.random.randint(jax.random.fold_in(jax.random.fold_in(_rk, 5), 23), (2048,), 32, 91694, jnp.int32), jax.random.randint(jax.random.fold_in(jax.random.fold_in(_rk, 5), 24), (2048,), 27, 91693, jnp.int32), jax.random.randint(jax.random.fold_in(jax.random.fold_in(_rk, 5), 25), (2048,), 1, 11463, jnp.int32), jax.random.randint(jax.random.fold_in(jax.random.fold_in(_rk, 5), 26), (2048,), 25, 91718, jnp.int32), jax.random.randint(jax.random.fold_in(jax.random.fold_in(_rk, 5), 27), (2048,), 9, 91718, jnp.int32), jax.random.randint(jax.random.fold_in(jax.random.fold_in(_rk, 5), 28), (2048,), 30, 91708, jnp.int32), jax.random.randint(jax.random.fold_in(jax.random.fold_in(_rk, 5), 29), (2048,), 1, 91694, jnp.int32), jax.random.randint(jax.random.fold_in(jax.random.fold_in(_rk, 5), 30), (2048,), 1, 91715, jnp.int32), jax.random.randint(jax.random.fold_in(jax.random.fold_in(_rk, 5), 31), (2048,), 12, 91674, jnp.int32), jax.random.randint(jax.random.fold_in(jax.random.fold_in(_rk, 5), 32), (2048,), 21, 91702, jnp.int32), jax.random.randint(jax.random.fold_in(jax.random.fold_in(_rk, 5), 33), (2048,), 5, 91716, jnp.int32), jax.random.randint(jax.random.fold_in(jax.random.fold_in(_rk, 5), 34), (2048,), 1, 91710, jnp.int32), jax.random.randint(jax.random.fold_in(jax.random.fold_in(_rk, 5), 35), (2048,), 3, 91714, jnp.int32), jax.random.randint(jax.random.fold_in(jax.random.fold_in(_rk, 5), 36), (2048,), 23, 11462, jnp.int32), jax.random.randint(jax.random.fold_in(jax.random.fold_in(_rk, 5), 37), (2048,), 6, 91706, jnp.int32), jax.random.randint(jax.random.fold_in(jax.random.fold_in(_rk, 5), 38), (2048,), 7, 91706, jnp.int32), jax.random.randint(jax.random.fold_in(jax.random.fold_in(_rk, 5), 39), (2048,), 23, 91705, jnp.int32), jax.random.randint(jax.random.fold_in(jax.random.fold_in(_rk, 5), 40), (2048,), 21, 91702, jnp.int32), jax.random.randint(jax.random.fold_in(jax.random.fold_in(_rk, 5), 41), (2048,), 7, 91714, jnp.int32), jax.random.randint(jax.random.fold_in(jax.random.fold_in(_rk, 5), 42), (2048,), 9, 91711, jnp.int32), jax.random.randint(jax.random.fold_in(jax.random.fold_in(_rk, 5), 43), (2048,), 15, 91702, jnp.int32), jax.random.randint(jax.random.fold_in(jax.random.fold_in(_rk, 5), 44), (2048,), 0, 91716, jnp.int32), jax.random.randint(jax.random.fold_in(jax.random.fold_in(_rk, 5), 45), (2048,), 8, 91713, jnp.int32), jax.random.randint(jax.random.fold_in(jax.random.fold_in(_rk, 5), 46), (2048,), 5, 91715, jnp.int32), jax.random.randint(jax.random.fold_in(jax.random.fold_in(_rk, 5), 47), (2048,), 28, 91710, jnp.int32), jax.random.randint(jax.random.fold_in(jax.random.fold_in(_rk, 5), 48), (2048,), 0, 91699, jnp.int32), jax.random.randint(jax.random.fold_in(jax.random.fold_in(_rk, 5), 49), (2048,), 43, 91689, jnp.int32)], axis=1)
        return (r_item_emb_d128, r_item_id, r_likes_level, r_views_level, r_item_seq)
    r_item_emb_d128, r_item_id, r_likes_level, r_views_level, r_item_seq = _rec_inputs()

    def _L0_rec_setup():
        import jax, jax.numpy as jnp
        import numpy as np
        EMB = 128
        NUM_FIELDS = 5
        TOTAL_DIM = (NUM_FIELDS + NUM_FIELDS * (NUM_FIELDS - 1) // 2) * EMB

        def _ln(x, g, b, eps=1e-05):
            m = jnp.mean(x, axis=-1, keepdims=True)
            v = jnp.mean(jnp.square(x - m), axis=-1, keepdims=True)
            return (x - m) * jax.lax.rsqrt(v + eps) * g + b

        def _forward(item_id, item_emb_d128, likes_level, views_level, item_seq, item_table, cate_table, mm_w, mm_b, mm_ln_g, mm_ln_b, aw1, ab1, aw2, ab2, se_w1, se_b1, se_w2, se_b2, bil_W, cross_K, cross_bias, w1, b1, ln1g, ln1b, w2, b2, ln2g, ln2b, w3, b3):
            B = item_id.shape[0]
            like_feat = cate_table[likes_level]
            view_feat = cate_table[views_level]
            item_id_feat = item_table[item_id]
            item_img_feat = jax.nn.gelu(_ln(item_emb_d128 @ mm_w + mm_b, mm_ln_g, mm_ln_b), approximate=False)
            target = item_id_feat + item_img_feat
            seq_emb = item_table[item_seq]
            mask = item_seq == 0
            t = jnp.broadcast_to(target[:, None, :], seq_emb.shape)
            x = jnp.concatenate([t, seq_emb, t - seq_emb, t * seq_emb], axis=-1)
            scores = (jax.nn.relu(x @ aw1 + ab1) @ aw2 + ab2)[..., 0]
            scores = jnp.where(mask, -1000000000.0, scores)
            weights = jax.nn.softmax(scores, axis=1)
            hist_feat = jnp.einsum('bs,bsd->bd', weights, seq_emb)
            sparse = jnp.stack([like_feat, view_feat, item_id_feat, item_img_feat, hist_feat], axis=1)
            z = jnp.mean(sparse, axis=-1)
            w = jax.nn.sigmoid(jax.nn.relu(z @ se_w1 + se_b1) @ se_w2 + se_b2)
            se = sparse * w[:, :, None]
            vids = jnp.einsum('bfd,fde->bfe', se[:, :4], bil_W)
            p = [vids[:, i] * se[:, j] for i in range(4) for j in range(i + 1, 5)]
            bil = jnp.stack(p, axis=1)
            dnn_in = jnp.concatenate([se.reshape(B, -1), bil.reshape(B, -1)], axis=1)
            xc = dnn_in
            for i in range(2):
                xc = dnn_in * (xc @ cross_K[i] + cross_bias[i]) + xc
            h = jax.nn.gelu(_ln(xc @ w1 + b1, ln1g, ln1b), approximate=False)
            h = jax.nn.gelu(_ln(h @ w2 + b2, ln2g, ln2b), approximate=False)
            logits = h @ w3 + b3
            return jax.nn.sigmoid(logits)[:, 0]
        key = jax.random.key(seed)
        ks = jax.random.split(key, 32)
        B, S = (1024, 50)
        d = {}
        d['item_id'] = jax.random.randint(ks[0], (B,), 0, 91718)
        d['item_emb_d128'] = jax.random.normal(ks[1], (B, EMB), jnp.float32)
        d['likes_level'] = jax.random.randint(ks[2], (B,), 0, 11)
        d['views_level'] = jax.random.randint(ks[3], (B,), 0, 11)
        d['item_seq'] = jax.random.randint(ks[4], (B, S), 0, 91718)
        d['item_table'] = (jax.random.normal(ks[5], (91718, EMB), jnp.float32) * 0.02).at[0].set(0.0)
        d['cate_table'] = jax.random.normal(ks[6], (11, EMB), jnp.float32) * 0.02
        d['mm_w'] = jax.random.normal(ks[7], (EMB, EMB), jnp.float32) * 0.05
        d['mm_b'] = jnp.zeros((EMB,), jnp.float32)
        d['mm_ln_g'] = jnp.ones((EMB,), jnp.float32)
        d['mm_ln_b'] = jnp.zeros((EMB,), jnp.float32)
        d['aw1'] = jax.random.normal(ks[8], (4 * EMB, 64), jnp.float32) * 0.04
        d['ab1'] = jnp.zeros((64,), jnp.float32)
        d['aw2'] = jax.random.normal(ks[9], (64, 1), jnp.float32) * 0.1
        d['ab2'] = jnp.zeros((1,), jnp.float32)
        d['se_w1'] = jax.random.normal(ks[10], (5, 2), jnp.float32) * 0.4
        d['se_b1'] = jnp.zeros((2,), jnp.float32)
        d['se_w2'] = jax.random.normal(ks[11], (2, 5), jnp.float32) * 0.4
        d['se_b2'] = jnp.zeros((5,), jnp.float32)
        d['bil_W'] = jax.random.normal(ks[12], (4, EMB, EMB), jnp.float32) * 0.09
        d['cross_K'] = jax.random.normal(ks[13], (2, TOTAL_DIM, TOTAL_DIM), jnp.float32) * 0.023
        d['cross_bias'] = jnp.zeros((2, TOTAL_DIM), jnp.float32)
        d['w1'] = jax.random.normal(ks[14], (TOTAL_DIM, 512), jnp.float32) * 0.02
        d['b1'] = jnp.zeros((512,), jnp.float32)
        d['ln1g'] = jnp.ones((512,), jnp.float32)
        d['ln1b'] = jnp.zeros((512,), jnp.float32)
        d['w2'] = jax.random.normal(ks[15], (512, 256), jnp.float32) * 0.04
        d['b2'] = jnp.zeros((256,), jnp.float32)
        d['ln2g'] = jnp.ones((256,), jnp.float32)
        d['ln2b'] = jnp.zeros((256,), jnp.float32)
        d['w3'] = jax.random.normal(ks[16], (256, 1), jnp.float32) * 0.06
        d['b3'] = jnp.zeros((1,), jnp.float32)
        return d
    _L0_rec_all = _L0_rec_setup()
    _L0_rec_in = {k: v for k, v in _L0_rec_all.items() if k in ('item_table', 'cate_table', 'mm_w', 'mm_b', 'mm_ln_g', 'mm_ln_b', 'aw1', 'ab1', 'aw2', 'ab2', 'se_w1', 'se_b1', 'se_w2', 'se_b2', 'bil_W', 'cross_K', 'cross_bias', 'w1', 'b1', 'ln1g', 'ln1b', 'w2', 'b2', 'ln2g', 'ln2b', 'w3', 'b3')}
    del _L0_rec_all
    return {'r_item_emb_d128': r_item_emb_d128, 'r_item_id': r_item_id, 'r_likes_level': r_likes_level, 'r_views_level': r_views_level, 'r_item_seq': r_item_seq, 'L0_rec_item_table': _L0_rec_in['item_table'], 'L0_rec_cate_table': _L0_rec_in['cate_table'], 'L0_rec_mm_w': _L0_rec_in['mm_w'], 'L0_rec_mm_b': _L0_rec_in['mm_b'], 'L0_rec_mm_ln_g': _L0_rec_in['mm_ln_g'], 'L0_rec_mm_ln_b': _L0_rec_in['mm_ln_b'], 'L0_rec_aw1': _L0_rec_in['aw1'], 'L0_rec_ab1': _L0_rec_in['ab1'], 'L0_rec_aw2': _L0_rec_in['aw2'], 'L0_rec_ab2': _L0_rec_in['ab2'], 'L0_rec_se_w1': _L0_rec_in['se_w1'], 'L0_rec_se_b1': _L0_rec_in['se_b1'], 'L0_rec_se_w2': _L0_rec_in['se_w2'], 'L0_rec_se_b2': _L0_rec_in['se_b2'], 'L0_rec_bil_W': _L0_rec_in['bil_W'], 'L0_rec_cross_K': _L0_rec_in['cross_K'], 'L0_rec_cross_bias': _L0_rec_in['cross_bias'], 'L0_rec_w1': _L0_rec_in['w1'], 'L0_rec_b1': _L0_rec_in['b1'], 'L0_rec_ln1g': _L0_rec_in['ln1g'], 'L0_rec_ln1b': _L0_rec_in['ln1b'], 'L0_rec_w2': _L0_rec_in['w2'], 'L0_rec_b2': _L0_rec_in['b2'], 'L0_rec_ln2g': _L0_rec_in['ln2g'], 'L0_rec_ln2b': _L0_rec_in['ln2b'], 'L0_rec_w3': _L0_rec_in['w3'], 'L0_rec_b3': _L0_rec_in['b3']}

def reference(r_item_emb_d128, r_item_id, r_likes_level, r_views_level, r_item_seq, L0_rec_item_table, L0_rec_cate_table, L0_rec_mm_w, L0_rec_mm_b, L0_rec_mm_ln_g, L0_rec_mm_ln_b, L0_rec_aw1, L0_rec_ab1, L0_rec_aw2, L0_rec_ab2, L0_rec_se_w1, L0_rec_se_b1, L0_rec_se_w2, L0_rec_se_b2, L0_rec_bil_W, L0_rec_cross_K, L0_rec_cross_bias, L0_rec_w1, L0_rec_b1, L0_rec_ln1g, L0_rec_ln1b, L0_rec_w2, L0_rec_b2, L0_rec_ln2g, L0_rec_ln2b, L0_rec_w3, L0_rec_b3):
    import jax
    import jax.numpy as jnp

    def _L0_rec_ref(item_id, item_emb_d128, likes_level, views_level, item_seq, item_table, cate_table, mm_w, mm_b, mm_ln_g, mm_ln_b, aw1, ab1, aw2, ab2, se_w1, se_b1, se_w2, se_b2, bil_W, cross_K, cross_bias, w1, b1, ln1g, ln1b, w2, b2, ln2g, ln2b, w3, b3):
        import jax, jax.numpy as jnp
        import numpy as np
        EMB = 128
        NUM_FIELDS = 5
        TOTAL_DIM = (NUM_FIELDS + NUM_FIELDS * (NUM_FIELDS - 1) // 2) * EMB

        def _ln(x, g, b, eps=1e-05):
            m = jnp.mean(x, axis=-1, keepdims=True)
            v = jnp.mean(jnp.square(x - m), axis=-1, keepdims=True)
            return (x - m) * jax.lax.rsqrt(v + eps) * g + b

        def _forward(item_id, item_emb_d128, likes_level, views_level, item_seq, item_table, cate_table, mm_w, mm_b, mm_ln_g, mm_ln_b, aw1, ab1, aw2, ab2, se_w1, se_b1, se_w2, se_b2, bil_W, cross_K, cross_bias, w1, b1, ln1g, ln1b, w2, b2, ln2g, ln2b, w3, b3):
            B = item_id.shape[0]
            like_feat = cate_table[likes_level]
            view_feat = cate_table[views_level]
            item_id_feat = item_table[item_id]
            item_img_feat = jax.nn.gelu(_ln(item_emb_d128 @ mm_w + mm_b, mm_ln_g, mm_ln_b), approximate=False)
            target = item_id_feat + item_img_feat
            seq_emb = item_table[item_seq]
            mask = item_seq == 0
            t = jnp.broadcast_to(target[:, None, :], seq_emb.shape)
            x = jnp.concatenate([t, seq_emb, t - seq_emb, t * seq_emb], axis=-1)
            scores = (jax.nn.relu(x @ aw1 + ab1) @ aw2 + ab2)[..., 0]
            scores = jnp.where(mask, -1000000000.0, scores)
            weights = jax.nn.softmax(scores, axis=1)
            hist_feat = jnp.einsum('bs,bsd->bd', weights, seq_emb)
            sparse = jnp.stack([like_feat, view_feat, item_id_feat, item_img_feat, hist_feat], axis=1)
            z = jnp.mean(sparse, axis=-1)
            w = jax.nn.sigmoid(jax.nn.relu(z @ se_w1 + se_b1) @ se_w2 + se_b2)
            se = sparse * w[:, :, None]
            vids = jnp.einsum('bfd,fde->bfe', se[:, :4], bil_W)
            p = [vids[:, i] * se[:, j] for i in range(4) for j in range(i + 1, 5)]
            bil = jnp.stack(p, axis=1)
            dnn_in = jnp.concatenate([se.reshape(B, -1), bil.reshape(B, -1)], axis=1)
            xc = dnn_in
            for i in range(2):
                xc = dnn_in * (xc @ cross_K[i] + cross_bias[i]) + xc
            h = jax.nn.gelu(_ln(xc @ w1 + b1, ln1g, ln1b), approximate=False)
            h = jax.nn.gelu(_ln(h @ w2 + b2, ln2g, ln2b), approximate=False)
            logits = h @ w3 + b3
            return jax.nn.sigmoid(logits)[:, 0]
        return _forward(item_id, item_emb_d128, likes_level, views_level, item_seq, item_table, cate_table, mm_w, mm_b, mm_ln_g, mm_ln_b, aw1, ab1, aw2, ab2, se_w1, se_b1, se_w2, se_b2, bil_W, cross_K, cross_bias, w1, b1, ln1g, ln1b, w2, b2, ln2g, ln2b, w3, b3)
    y = _L0_rec_ref(r_item_id, r_item_emb_d128, r_likes_level, r_views_level, r_item_seq, L0_rec_item_table, L0_rec_cate_table, L0_rec_mm_w, L0_rec_mm_b, L0_rec_mm_ln_g, L0_rec_mm_ln_b, L0_rec_aw1, L0_rec_ab1, L0_rec_aw2, L0_rec_ab2, L0_rec_se_w1, L0_rec_se_b1, L0_rec_se_w2, L0_rec_se_b2, L0_rec_bil_W, L0_rec_cross_K, L0_rec_cross_bias, L0_rec_w1, L0_rec_b1, L0_rec_ln1g, L0_rec_ln1b, L0_rec_w2, L0_rec_b2, L0_rec_ln2g, L0_rec_ln2b, L0_rec_w3, L0_rec_b3)
    return y

_drawn_inputs = setup_inputs


def setup_inputs(seed=0):
    import zlib

    import numpy as np

    out = dict(_drawn_inputs(seed))
    spreads = {'L0_rec_mm_b': (0.0, 0.1),
     'L0_rec_mm_ln_g': (1.0, 0.2),
     'L0_rec_mm_ln_b': (0.0, 0.1),
     'L0_rec_ab1': (0.0, 0.8),
     'L0_rec_se_b1': (0.0, 0.8),
     'L0_rec_se_b2': (0.0, 0.8),
     'L0_rec_cross_bias': (0.0, 0.1),
     'L0_rec_b1': (0.0, 0.1),
     'L0_rec_ln1g': (1.0, 0.2),
     'L0_rec_ln1b': (0.0, 0.3),
     'L0_rec_b2': (0.0, 0.1),
     'L0_rec_ln2g': (1.0, 0.2),
     'L0_rec_ln2b': (0.0, 0.368)}
    factors = {'L0_rec_item_table': 6.218,
     'L0_rec_cate_table': 4.644,
     'L0_rec_aw1': 8.0,
     'L0_rec_aw2': 8.0,
     'L0_rec_se_w1': 8.0,
     'L0_rec_se_w2': 8.0,
     'L0_rec_bil_W': 8.0}
    for name, (base, spread) in spreads.items():
        noise = np.random.default_rng([zlib.crc32(name.encode()), seed]).standard_normal(out[name].shape)
        drawn = base * np.exp(spread * noise) if base else spread * noise
        out[name] = jnp.asarray(drawn.astype(out[name].dtype))
    for name, factor in factors.items():
        out[name] = (out[name] * factor).astype(out[name].dtype)
    return out
```

```python
from contextlib import ExitStack

import concourse.bass as bass
from concourse import mybir

ALU = mybir.AluOpType
ACT = mybir.ActivationFunctionType
AX = mybir.AxisListType
F32 = mybir.dt.float32
F32R = mybir.dt.float32r
I32 = mybir.dt.int32

P = 128
EMB = 128
SEQ = 50
HID = 64
FIELDS = 5
FEATS = FIELDS + FIELDS * (FIELDS - 1) // 2
TPC = 4
NB = TPC * P
GRP = 10
SUB = 5
NG = SEQ // GRP
KG = 5
UNITS = FEATS // KG
H1 = 512
H2 = 256
RING = 3
BANKS = 3
EPS = 1e-5
LEAST = -3.0e38
MASKED = -1.0e9
DMA = 16

ROWS = {}
_at = 0
for _name, _n in (("mm_b", EMB), ("mm_g", EMB), ("mm_lb", EMB), ("ab1", HID), ("aw2", HID), ("b1", H1),
                  ("b2", H2), ("se_w1", 2 * FIELDS), ("se_b1", 2), ("se_w2", 2 * FIELDS), ("se_b2", FIELDS),
                  ("ab2", 1), ("b3", 1)):
    ROWS[_name] = (_at, _at + _n)
    _at += _n
NROWS = _at
COLS = {}
_at = 0
for _name, _n in (("g1", 4), ("lb1", 4), ("g2", 2), ("lb2", 2), ("w3", 2), ("cb", 2 * FEATS)):
    COLS[_name] = (_at, _at + _n)
    _at += _n
NCOLS = _at

SEGMENTS = [(0, 1, 0, None, 1), (0, 2, 1, 0, 2), (1, 0, 2, 1, 3), (1, 1, 3, 2, None), (1, 2, None, 3, None)]


def link(eng, sem, ins):
    ins.then_inc(sem, 1)
    eng.wait_ge(sem, 1).then_inc(sem, -1)


def build(nc, idx_d, table_d, cate_d, embT_d, rows_d, cols_d, mmw_d, aw1_d, bil_d, kx_d, w1_d, w2_d, out_d, ntiles):
    nchunks = ntiles // TPC
    with ExitStack() as ctx:
        def sb(name, shape, dt=F32):
            return ctx.enter_context(nc.sbuf_tensor(name, shape, dt))

        def ps(name, shape):
            return ctx.enter_context(nc.psum_tensor(name, shape, F32))

        def sem(name):
            return ctx.enter_context(nc.semaphore(name))

        dnn_d = nc.dram_tensor("dnn_scratch", (nchunks, FEATS, P, TPC, P), F32, kind="Internal").ap()

        xps = ps("xps", [P, BANKS + 1, 512])
        FCB = BANKS
        tps = ps("tps", [P, 2 * 512])
        hps = ps("hps", [P, 512])
        mps = ps("mps", [P, 512])

        X0h = sb("X0h", [P, FEATS, NB], F32R)
        X0l = sb("X0l", [P, FEATS, NB], F32R)
        X1h = sb("X1h", [P, FEATS, NB], F32R)
        X1l = sb("X1l", [P, FEATS, NB], F32R)
        raw = sb("raw", [P, RING, KG * P])
        Wh = sb("Wh", [P, RING, KG * P], F32R)
        Wl = sb("Wl", [P, RING, KG * P], F32R)
        xnew = sb("xnew", [P, NB])
        e = sb("e", [P, NG * GRP, EMB])
        eT = sb("eT", [P, SUB, P])
        teT = sb("teT", [P, SUB, P])
        idx_all = sb("idx_all", [P, ntiles, SEQ + 3], I32)
        idx_cur = sb("idx_cur", [P, 2, SEQ + 3], I32)
        S = sb("S", [P, 2, FIELDS, EMB])
        tT = sb("tT", [P, 2, P])
        Tt = sb("Tt", [P, 2, HID])
        keep = sb("keep", [P, 2, SEQ])
        mbias = sb("mbias", [P, 2, SEQ])
        hid = sb("hid", [P, SUB, HID])
        sc = sb("sc", [P, GRP])
        pw = sb("pw", [P, GRP])
        gmax = sb("gmax", [P, 1])
        rmax = sb("rmax", [P, 1])
        nmax = sb("nmax", [P, 1])
        corr = sb("corr", [P, 1])
        gsum = sb("gsum", [P, 1])
        rsum = sb("rsum", [P, 1])
        rinv = sb("rinv", [P, 1])
        acc = sb("acc", [P, EMB])
        emb4 = sb("emb4", [P, NB])
        xi = sb("xi", [P, EMB])
        tgt = sb("tgt", [P, EMB])
        stats = sb("stats", [P, 6])
        mv = sb("mv", [P, 2])
        sd = sb("sd", [P, 1])
        rstd = sb("rstd", [P, 1])
        fstats = sb("fstats", [P, 6])
        fmv = sb("fmv", [P, 2])
        fsd = sb("fsd", [P, 1])
        frstd = sb("frstd", [P, 1])
        z5 = sb("z5", [P, FIELDS])
        se10 = sb("se10", [P, 2 * FIELDS])
        se2 = sb("se2", [P, 2])
        g5 = sb("g5", [P, FIELDS])
        dn = sb("dn", [P, TPC * H1 // P, P])
        h1 = dn[:].rearrange("p f b -> p (f b)").rearrange("p (t n) -> p t n", t=TPC)
        fbuf = sb("fbuf", [P, H1])
        h1n = fbuf
        g1T = fbuf[:].rearrange("p (k b) -> p k b", b=P)
        h2 = fbuf[:, 0:H2]
        g2T = fbuf[:, 0:H2].rearrange("p (k b) -> p k b", b=P)
        logits = sb("logits", [P, TPC * (nchunks + 1)])
        probs = sb("probs", [P, ntiles])
        res = sb("res", [ntiles, P])
        ident = sb("ident", [P, P])
        eps = sb("eps", [P, 1])
        rows = sb("rows", [P, NROWS])
        cols = sb("cols", [P, NCOLS])
        mmw = sb("mmw", [P, EMB])
        aw1 = sb("aw1", [P, 4, HID])
        A02 = sb("A02", [P, HID])
        A12 = sb("A12", [P, HID])
        bil = sb("bil", [P, 4, EMB])
        w2 = sb("w2", [P, H1 // P, H2])

        def row(name):
            a, b = ROWS[name]
            return rows[:, a:b]

        def col(name, k, n=1):
            a, _ = COLS[name]
            return cols[:, a + k:a + k + n]

        consts_in = sem("consts_in")
        consts_ok = sem("consts_ok")
        ident_ok = sem("ident_ok")
        ident_z = sem("ident_z")
        idx_in = sem("idx_in")
        act_done = sem("act_done")
        dve_done = sem("dve_done")
        pool_done = sem("pool_done")
        raw_landed = [sem(f"raw_landed{i}") for i in range(RING)]
        raw_free = sem("raw_free")
        split_free = sem("split_free")
        hi_done = sem("hi_done")
        w_ready = sem("w_ready")
        x_ready = sem("x_ready")
        x0_free = sem("x0_free")
        bank_free = sem("bank_free")
        mm_done = sem("mm_done")
        xnew_ready = sem("xnew_ready")
        xhi_done = sem("xhi_done")
        emb_landed = sem("emb_landed")
        emb_free = sem("emb_free")
        dnn_stored = sem("dnn_stored")
        dnn_ready = sem("dnn_ready")
        feat_landed = [sem(f"feat_landed{i}") for i in range(2)]
        e_landed = [sem(f"e_landed{i}") for i in range(NG)]
        e_free = sem("e_free")
        S_free = sem("S_free")
        tp_ready = sem("tp_ready")
        tp_free = sem("tp_free")
        eT_ready = sem("eT_ready")
        eT_free = sem("eT_free")
        te_ready = sem("te_ready")
        h_ready = sem("h_ready")
        h_free = sem("h_free")
        sc_ready = sem("sc_ready")
        p_ready = sem("p_ready")
        pe_ready = sem("pe_ready")
        m_free = sem("m_free")
        m_ready = sem("m_ready")
        var_ready = sem("var_ready")
        sd_ready = sem("sd_ready")
        xi_ready = sem("xi_ready")
        img_ready = sem("img_ready")
        tgt_ready = sem("tgt_ready")
        tT_ready = sem("tT_ready")
        gate_ready = sem("gate_ready")
        gexp_ready = sem("gexp_ready")
        se_ready = sem("se_ready")
        seT_ready = sem("seT_ready")
        dn_full = sem("dn_full")
        fc_free = sem("fc_free")
        h1n_ready = sem("h1n_ready")
        fvar_ready = sem("fvar_ready")
        fsd_ready = sem("fsd_ready")
        fT_ready = sem("fT_ready")
        g_ready = sem("g_ready")
        fmm_ready = sem("fmm_ready")
        h2n_ready = sem("h2n_ready")
        logits_ready = sem("logits_ready")
        lexp_ready = sem("lexp_ready")
        probs_ready = sem("probs_ready")
        probsT_ready = sem("probsT_ready")
        res_ready = sem("res_ready")
        out_stored = sem("out_stored")

        NCONST = 6

        UL = FEATS * UNITS
        START = 2 + FEATS - 1
        R14_SLOT = START % RING

        def w_slot(q):
            return (q + 2) % RING

        def w1_slots(k, refill):
            at = START + 2 * UL + 1 + (2 * k - 1 if refill and k else k)
            return at % RING, (at + 1) % RING

        def e_sub(g, u, s):
            return e[:, g * GRP + u * SUB + s, :]

        block = ctx.enter_context(nc.Block())

        @block.sync
        def _(sp):
            def load(slot, src, n):
                sp.wait_ge(raw_free, 1).then_inc(raw_free, -1)
                sp.dma_start(raw[:, slot, 0:n], src).then_inc(raw_landed[slot], DMA)

            def k_unit(u, slot):
                load(slot, kx_d[u], KG * P)

            def w1_unit(k, slot):
                load(slot, w1_d[k * P:(k + 1) * P, :], H1)

            def r_unit(c, k, slot):
                load(slot, dnn_d[c, k].rearrange("p t b -> p (t b)"), NB)

            def emb_load(c):
                sp.wait_ge(emb_free, 1).then_inc(emb_free, -1)
                sp.dma_start(emb4[:], embT_d[:, bass.ds(c * NB, NB)]).then_inc(emb_landed, DMA)

            sp.dma_start(idx_all[:], idx_d).then_inc(idx_in, DMA)
            emb_load(0)
            sp.dma_start(mmw[:], mmw_d).then_inc(consts_in, DMA)
            sp.dma_start(rows[:], rows_d).then_inc(consts_in, DMA)
            sp.dma_start(cols[:], cols_d).then_inc(consts_in, DMA)
            sp.dma_start(aw1[:], aw1_d.rearrange("(q p) n -> p q n", p=P)).then_inc(consts_in, DMA)
            sp.dma_start(bil[:], bil_d.rearrange("i d e -> d i e")).then_inc(consts_in, DMA)
            sp.dma_start(w2[:], w2_d.rearrange("(k p) n -> p k n", p=P)).then_inc(consts_in, DMA)
            k_unit(0, 0)
            k_unit(1, 1)
            sp.wait_ge(dnn_ready, TPC).then_inc(dnn_ready, -TPC)
            for k in range(FEATS - 1):
                r_unit(0, k, (2 + k) % RING)

            def chunk(c, more):
                if more:
                    emb_load(c + 1)
                r_unit(c, FEATS - 1, R14_SLOT)
                with sp.Fori(0, (2 * UL - 3) // RING) as i:
                    for j in range(RING):
                        k_unit(i * RING + 2 + j, (2 + j) % RING)
                k_unit(2 * UL - 1, (2 * UL - 1) % RING)
                w1_unit(0, w_slot(2 * UL - 2))
                w1_unit(1, w_slot(2 * UL - 1))
                for k in range(FEATS):
                    ws, rs = w1_slots(k, more)
                    if k + 2 < FEATS:
                        w1_unit(k + 2, ws)
                    elif more:
                        k_unit(k + 2 - FEATS, ws)
                    if more and k:
                        if k == 1:
                            sp.wait_ge(dnn_ready, TPC).then_inc(dnn_ready, -TPC)
                        r_unit(c + 1, k - 1, rs)

            with sp.Fori(0, nchunks - 1) as c:
                chunk(c, True)
            chunk(nchunks - 1, False)
            sp.wait_ge(res_ready, 1).then_inc(res_ready, -1)
            sp.dma_start(out_d, res[:]).then_inc(out_stored, DMA)
            sp.wait_ge(out_stored, DMA)

        @block.gpsimd
        def _(pool):
            nc.gpsimd.memset(ident[:], 0.0).then_inc(ident_z, 1)
            pool.wait_ge(ident_z, 1).then_inc(ident_z, -1)
            nc.gpsimd.affine_select(out=ident[:], in_=ident[:], compare_op=ALU.not_equal, fill=1.0, base=0,
                                    pattern=[[-1, P]], channel_multiplier=1).then_inc(ident_ok, 1)
            pool.wait_ge(idx_in, DMA)

            def gather(dst, table, par, s, landed):
                nc.gpsimd.indirect_dma_start(
                    out=dst, out_offset=None, in_=table,
                    in_offset=bass.IndirectOffsetOnAxis(ap=idx_cur[:, par, s:s + 1], axis=0),
                ).then_inc(landed, DMA)

            with pool.Fori(0, ntiles // 2) as i:
                for par in range(2):
                    pool.wait_ge(S_free, 1).then_inc(S_free, -1)
                    link(pool, pool_done, nc.gpsimd.tensor_copy(idx_cur[:, par, :], idx_all[:, i * 2 + par, :]))
                    gather(S[:, par, 2, :], table_d, par, SEQ, feat_landed[par])
                    gather(S[:, par, 0, :], cate_d, par, SEQ + 1, feat_landed[par])
                    gather(S[:, par, 1, :], cate_d, par, SEQ + 2, feat_landed[par])
                    for g in range(NG):
                        pool.wait_ge(e_free, 1).then_inc(e_free, -1)
                        for s in range(GRP):
                            gather(e[:, g * GRP + s, :], table_d, par, g * GRP + s, e_landed[g])

        @block.tensor
        def _(pe):
            mm = nc.tensor.matmul

            def transposes(t, g, u):
                if u == 0:
                    pe.wait_ge(e_landed[g], (t + 1) * (DMA * GRP))
                pe.wait_ge(tp_free, 1).then_inc(tp_free, -1)
                for s in range(SUB):
                    last = nc.tensor.transpose(tps[:, s * P:(s + 1) * P], e_sub(g, u, s), ident[:])
                last.then_inc(tp_ready, 1)

            def hidden(par):
                pe.wait_ge(te_ready, 1).then_inc(te_ready, -1)
                pe.wait_ge(h_free, 1).then_inc(h_free, -1)
                for s in range(SUB):
                    o = hps[:, s * HID:(s + 1) * HID]
                    mm(o, eT[:, s, :], A12[:], start=True, stop=False)
                    last = mm(o, teT[:, s, :], aw1[:, 3, :], start=False, stop=True)
                last.then_inc(h_ready, 1)

            def head_mm(j):
                if j == 0:
                    pe.wait_ge(emb_landed, DMA).then_inc(emb_landed, -DMA)
                pe.wait_ge(m_free, 1).then_inc(m_free, -1)
                mm(mps[:, 0:P], emb4[:, j * P:(j + 1) * P], mmw[:], start=True, stop=True).then_inc(m_ready, 1)

            def head_turn():
                pe.wait_ge(tgt_ready, 1).then_inc(tgt_ready, -1)
                pe.wait_ge(m_free, 1).then_inc(m_free, -1)
                nc.tensor.transpose(mps[:, 0:P], tgt[:], ident[:]).then_inc(m_ready, 1)

            def head_share(par):
                pe.wait_ge(tT_ready, 1).then_inc(tT_ready, -1)
                mm(mps[:, P:P + HID], tT[:, par, :], A02[:], start=True, stop=True).then_inc(m_ready, 1)

            def tail_turn(par):
                pe.wait_ge(se_ready, 1).then_inc(se_ready, -1)
                pe.wait_ge(tp_free, 1).then_inc(tp_free, -1)
                for f in range(FIELDS):
                    last = nc.tensor.transpose(tps[:, f * P:(f + 1) * P], S[:, par, f, :], ident[:])
                last.then_inc(tp_ready, 1)

            def tail_bilinear():
                pe.wait_ge(seT_ready, 1).then_inc(seT_ready, -1)
                pe.wait_ge(m_free, 1).then_inc(m_free, -1)
                for i in range(4):
                    last = mm(mps[:, i * P:(i + 1) * P], bil[:, i, :], dn[:, i, :], start=True, stop=True)
                last.then_inc(m_ready, 1)

            def products(layer, n, kg, first):
                Xh, Xl = (X0h, X0l) if layer == 0 else (X1h, X1l)
                out = xps[:, n % BANKS, :]
                if kg == 0:
                    pe.wait_ge(bank_free, 1).then_inc(bank_free, -1)
                pe.wait_ge(w_ready, 1).then_inc(w_ready, -1)
                for i in range(KG):
                    k = kg * KG + i
                    if first:
                        pe.wait_ge(x_ready, 1).then_inc(x_ready, -1)
                    wh, wl = Wh[:, kg, i * P:(i + 1) * P], Wl[:, kg, i * P:(i + 1) * P]
                    m0 = mm(out, wh, Xh[:, k, :], start=(k == 0), stop=False)
                    m1 = mm(out, wh, Xl[:, k, :], start=False, stop=False)
                    m2 = mm(out, wl, Xh[:, k, :], start=False, stop=(k == FEATS - 1))
                    if i == 0:
                        m0.then_inc(split_free, 1)
                        if layer == 0 and first and kg == 0:
                            m1.then_inc(x0_free, 1)
                if kg == UNITS - 1:
                    m2.then_inc(mm_done, 1)

            def w1_products(more):
                for _ in range(BANKS):
                    pe.wait_ge(bank_free, 1).then_inc(bank_free, -1)
                pe.wait_ge(fc_free, 1).then_inc(fc_free, -1)
                for k in range(FEATS):
                    pe.wait_ge(w_ready, 1).then_inc(w_ready, -1)
                    pe.wait_ge(x_ready, 1).then_inc(x_ready, -1)
                    s = k % RING
                    for b in range(TPC):
                        out = xps[:, b, :]
                        xh, xl = X0h[:, k, b * P:(b + 1) * P], X0l[:, k, b * P:(b + 1) * P]
                        m0 = mm(out, xh, Wh[:, s, 0:H1], start=(k == 0), stop=False)
                        m1 = mm(out, xh, Wl[:, s, 0:H1], start=False, stop=False)
                        m2 = mm(out, xl, Wh[:, s, 0:H1], start=False, stop=(k == FEATS - 1))
                        if b == 0:
                            m0.then_inc(split_free, 1)
                            if more and k:
                                m1.then_inc(x0_free, 1)
                m2.then_inc(mm_done, 1)

            def fc_turn1():
                pe.wait_ge(h1n_ready, 1).then_inc(h1n_ready, -1)
                pe.wait_ge(fc_free, 1).then_inc(fc_free, -1)
                for k in range(H1 // P):
                    last = nc.tensor.transpose(xps[:, FCB, k * P:(k + 1) * P], h1n[:, k * P:(k + 1) * P], ident[:])
                last.then_inc(fT_ready, 1)

            def fc_w2():
                pe.wait_ge(g_ready, 1).then_inc(g_ready, -1)
                pe.wait_ge(fc_free, 1).then_inc(fc_free, -1)
                for k in range(H1 // P):
                    last = mm(xps[:, FCB, 0:H2], g1T[:, k, :], w2[:, k, :], start=(k == 0), stop=(k == H1 // P - 1))
                last.then_inc(fmm_ready, 1)

            def fc_turn2():
                pe.wait_ge(h2n_ready, 1).then_inc(h2n_ready, -1)
                pe.wait_ge(fc_free, 1).then_inc(fc_free, -1)
                for k in range(H2 // P):
                    last = nc.tensor.transpose(xps[:, FCB, k * P:(k + 1) * P], h2[:, k * P:(k + 1) * P], ident[:])
                last.then_inc(fT_ready, 1)

            def fc_w3():
                pe.wait_ge(g_ready, 1).then_inc(g_ready, -1)
                pe.wait_ge(fc_free, 1).then_inc(fc_free, -1)
                for k in range(H2 // P):
                    last = mm(xps[:, FCB, 0:1], g2T[:, k, :], col("w3", k), start=(k == 0), stop=(k == H2 // P - 1))
                last.then_inc(fmm_ready, 1)

            def fc_step(n, first, logit):
                if logit:
                    fc_w3()
                products(0, n, 0, first)
                fc_turn1()
                products(0, n, 1, first)
                fc_w2()
                products(0, n, 2, first)
                fc_turn2()

            def fc_steps():
                fc_step(0, True, False)
                with pe.Fori(1, TPC) as n:
                    fc_step(n, False, True)

            def chunk(c, more):
                fc_steps()
                n = TPC
                fc_w3()
                if more:
                    head_mm(0)
                products(0, n, 0, False)
                products(0, n, 1, False)
                if more:
                    head_turn()
                products(0, n, 2, False)
                if more:
                    head_share(0)
                    for layer, third, grp, tail, head in SEGMENTS:
                        for i in range(5):
                            n = 5 * third + i
                            first = n == 0
                            if grp is not None:
                                transposes((c + 1) * TPC + grp, i, 0)
                            if tail is not None and i == 1:
                                tail_bilinear()
                            products(layer, n, 0, first)
                            if grp is not None:
                                hidden(grp % 2)
                                transposes((c + 1) * TPC + grp, i, 1)
                            products(layer, n, 1, first)
                            if grp is not None:
                                hidden(grp % 2)
                            if tail is not None and i == 0:
                                tail_turn(tail % 2)
                            if head is not None and i == 0:
                                head_mm(head)
                            if head is not None and i == 1:
                                head_turn()
                            products(layer, n, 2, first)
                            if head is not None and i == 1:
                                head_share(head % 2)
                else:
                    with pe.Fori(TPC + 1, FEATS) as n:
                        for kg in range(UNITS):
                            products(0, n, kg, False)
                    for kg in range(UNITS):
                        products(1, 0, kg, True)
                    with pe.Fori(1, FEATS) as n:
                        for kg in range(UNITS):
                            products(1, n, kg, False)
                w1_products(more)

            pe.wait_ge(ident_ok, 1)
            pe.wait_ge(consts_ok, 1)
            with pe.Fori(0, TPC // 2) as i:
                for par in range(2):
                    pe.wait_ge(m_free, 1).then_inc(m_free, -1)
                    pe.wait_ge(tgt_ready, 1).then_inc(tgt_ready, -1)
                    mm(mps[:, 0:P], tgt[:], mmw[:], start=True, stop=True).then_inc(m_ready, 1)
                    head_turn()
                    head_share(par)
                    for g in range(NG):
                        transposes(i * 2 + par, g, 0)
                        hidden(par)
                        transposes(i * 2 + par, g, 1)
                        hidden(par)
                    tail_turn(par)
                    tail_bilinear()
            with pe.Fori(0, nchunks - 1) as c:
                chunk(c, True)
            chunk(nchunks - 1, False)
            for j in range(TPC):
                fc_turn1()
                fc_w2()
                fc_turn2()
                fc_w3()
            pe.wait_ge(probs_ready, 1).then_inc(probs_ready, -1)
            pe.wait_ge(fc_free, 1).then_inc(fc_free, -1)
            nc.tensor.transpose(xps[0:ntiles, FCB, 0:P], probs[:, :], ident[:]).then_inc(probsT_ready, 1)

        @block.scalar
        def _(act):
            af = nc.scalar.activation

            def done(ins):
                link(act, act_done, ins)

            def copy_eT():
                act.wait_ge(tp_ready, 1).then_inc(tp_ready, -1)
                act.wait_ge(eT_free, 1).then_inc(eT_free, -1)
                done(af(eT[:].rearrange("p s b -> p (s b)"), tps[:, 0:SUB * P], ACT.Copy))
                act.sem_inc(tp_free, 1)
                act.sem_inc(eT_ready, 1)

            def exps():
                act.wait_ge(sc_ready, 1).then_inc(sc_ready, -1)
                done(af(corr[:], rmax[:], ACT.Exp, bias=nmax[:]))
                done(af(pw[:], sc[:], ACT.Exp, bias=nmax[:], accum_out=gsum[:]))
                act.sem_inc(p_ready, 1)

            def weigh(g):
                for s in range(GRP):
                    x = e[:, g * GRP + s, :]
                    last = af(x, x, ACT.Copy, scale=pw[:, s:s + 1])
                last.then_inc(pe_ready, 1)

            def head_sd():
                act.wait_ge(var_ready, 1).then_inc(var_ready, -1)
                af(sd[:], mv[:, 1:2], ACT.Sqrt, bias=eps[:]).then_inc(sd_ready, 1)

            def head_gelu(par):
                act.wait_ge(xi_ready, 1).then_inc(xi_ready, -1)
                af(S[:, par, 3, :], xi[:], ACT.Gelu).then_inc(img_ready, 1)

            def tail_gate():
                act.wait_ge(gate_ready, 1).then_inc(gate_ready, -1)
                af(g5[:], g5[:], ACT.Exp, scale=-1.0).then_inc(gexp_ready, 1)

            def tail_copy():
                act.wait_ge(tp_ready, 1).then_inc(tp_ready, -1)
                done(af(dn[:, 0:FIELDS, :].rearrange("p s b -> p (s b)"), tps[:, 0:FIELDS * P], ACT.Copy))
                act.sem_inc(tp_free, 1)
                act.sem_inc(S_free, 1)
                act.sem_inc(seT_ready, 1)

            def tail_store(c, j):
                act.wait_ge(dn_full, 1).then_inc(dn_full, -1)
                act.dma_start(dnn_d[c, :, :, j, :].rearrange("f p b -> p f b"), dn[:, 0:FEATS, :]).then_inc(dnn_stored, DMA)

            def tail_settle():
                act.wait_ge(dnn_stored, DMA).then_inc(dnn_stored, -DMA)
                act.sem_inc(dnn_ready, 1)

            def w_hi(raw_slot, slot, n=KG * P):
                act.wait_ge(raw_landed[raw_slot], DMA).then_inc(raw_landed[raw_slot], -DMA)
                act.wait_ge(split_free, 1).then_inc(split_free, -1)
                af(Wh[:, slot, 0:n], raw[:, raw_slot, 0:n], ACT.Copy).then_inc(hi_done, 1)

            def r_hi(raw_slot, k, reused=True):
                act.wait_ge(raw_landed[raw_slot], DMA).then_inc(raw_landed[raw_slot], -DMA)
                if reused:
                    act.wait_ge(x0_free, 1).then_inc(x0_free, -1)
                af(X0h[:, k, :], raw[:, raw_slot, 0:NB], ACT.Copy).then_inc(hi_done, 1)

            def x_hi(layer, n):
                act.wait_ge(xnew_ready, 1).then_inc(xnew_ready, -1)
                Xh = X1h if layer == 0 else X0h
                af(Xh[:, n, :], xnew[:], ACT.Copy).then_inc(xhi_done, 1)

            def fc_sd():
                act.wait_ge(fvar_ready, 1).then_inc(fvar_ready, -1)
                af(fsd[:], fmv[:, 1:2], ACT.Sqrt, bias=eps[:]).then_inc(fsd_ready, 1)

            def fc_gelu(dst, g, b, n):
                act.wait_ge(fT_ready, 1).then_inc(fT_ready, -1)
                for k in range(n):
                    last = af(dst[:, k, :], xps[:, FCB, k * P:(k + 1) * P], ACT.Gelu, scale=col(g, k), bias=col(b, k))
                done(last)
                act.sem_inc(fc_free, 1)
                act.sem_inc(g_ready, 1)

            def unit(q, last_layer):
                w_hi(w_slot(q), (q + 2) % RING, H1 if last_layer and q > 0 else KG * P)

            def fc_step(n, first):
                if first:
                    r_hi(R14_SLOT, FEATS - 1)
                fc_sd()
                unit(0, False)
                if not first:
                    x_hi(0, n - 1)
                fc_gelu(g1T, "g1", "lb1", H1 // P)
                unit(1, False)
                unit(2, False)
                fc_sd()
                fc_gelu(g2T, "g2", "lb2", H2 // P)

            def plain_step(layer, n, pending, last=False):
                unit(0, False)
                if pending is not None:
                    x_hi(pending, n - 1 if pending == layer else FEATS - 1)
                unit(1, last)
                unit(2, last)

            def w1_stage(more):
                for k in range(FEATS):
                    ws, rs = w1_slots(k, more)
                    if k + 2 < FEATS:
                        w_hi(ws, (k + 2) % RING, H1)
                    elif more:
                        w_hi(ws, (k + 2) % RING)
                    if k == 0:
                        x_hi(1, FEATS - 1)
                    if more and k:
                        r_hi(rs, k - 1)

            def chunk(c, more):
                fc_step(0, True)
                with act.Fori(1, TPC) as n:
                    fc_step(n, False)
                n = TPC
                unit(0, False)
                if more:
                    head_sd()
                x_hi(0, n - 1)
                if more:
                    head_gelu(0)
                unit(1, False)
                unit(2, False)
                if more:
                    for layer, third, grp, tail, head in SEGMENTS:
                        for i in range(5):
                            n = 5 * third + i
                            last = layer == 1 and n == FEATS - 1
                            if grp is not None:
                                copy_eT()
                            unit(0, False)
                            x_hi(*((layer, n - 1) if n else (0, FEATS - 1)))
                            if tail is not None and i == 1:
                                tail_store(c + 1, tail)
                            if head is not None and i == 1:
                                head_sd()
                                head_gelu(head % 2)
                            if grp is not None:
                                copy_eT()
                            if tail is not None and i == 0:
                                tail_gate()
                            unit(1, last)
                            unit(2, last)
                            if tail is not None and i == 0:
                                tail_copy()
                            if tail is not None and i == 2:
                                tail_settle()
                            if grp is not None:
                                exps()
                                weigh(i)
                else:
                    with act.Fori(TPC + 1, FEATS) as n:
                        plain_step(0, n, 0)
                    plain_step(1, 0, 0)
                    with act.Fori(1, FEATS - 1) as n:
                        plain_step(1, n, 1)
                    plain_step(1, FEATS - 1, 1, True)
                w1_stage(more)

            act.sem_inc(S_free, 2)
            act.sem_inc(tp_free, 1)
            act.wait_ge(consts_ok, 1).then_inc(consts_ok, -1)
            for u in range(2):
                act.wait_ge(raw_landed[u], DMA).then_inc(raw_landed[u], -DMA)
                af(Wh[:, u, :], raw[:, u, :], ACT.Copy).then_inc(hi_done, 1)
            with act.Fori(0, TPC // 2) as i:
                for par in range(2):
                    head_sd()
                    head_gelu(par)
                    for g in range(NG):
                        copy_eT()
                        copy_eT()
                        exps()
                        weigh(g)
                    tail_gate()
                    tail_copy()
                    tail_store(0, i * 2 + par)
                    tail_settle()
            for k in range(FEATS - 1):
                r_hi((2 + k) % RING, k, False)
            with act.Fori(0, nchunks - 1) as c:
                chunk(c, True)
            chunk(nchunks - 1, False)
            for j in range(TPC):
                fc_sd()
                fc_gelu(g1T, "g1", "lb1", H1 // P)
                fc_sd()
                fc_gelu(g2T, "g2", "lb2", H2 // P)
            act.wait_ge(logits_ready, 1).then_inc(logits_ready, -1)
            af(probs[:], logits[:, TPC:TPC + ntiles], ACT.Exp, scale=-1.0).then_inc(lexp_ready, 1)

        @block.vector
        def _(dve):
            v = nc.vector

            def done(ins):
                link(dve, dve_done, ins)

            def head_mask(par, t):
                done(v.tensor_scalar(keep[:, par, :], idx_all[:, t, 0:SEQ], 0.0, None, ALU.not_equal))
                done(v.tensor_scalar(mbias[:, par, :], idx_all[:, t, 0:SEQ], 0.0, MASKED, ALU.is_equal, ALU.mult))

            def head_var():
                dve.wait_ge(m_ready, 1).then_inc(m_ready, -1)
                done(v.tensor_tensor(xi[:], mps[:, 0:P], row("mm_b"), ALU.add))
                dve.sem_inc(m_free, 1)
                done(v.bn_stats(stats[:], xi[:]))
                done(v.bn_aggr(mv[:], stats[:]))
                dve.sem_inc(var_ready, 1)

            def head_norm():
                dve.wait_ge(sd_ready, 1).then_inc(sd_ready, -1)
                done(v.reciprocal(rstd[:], sd[:]))
                done(v.tensor_scalar(xi[:], xi[:], mv[:, 0:1], rstd[:], ALU.subtract, ALU.mult))
                done(v.tensor_tensor(xi[:], xi[:], row("mm_g"), ALU.mult))
                done(v.tensor_tensor(xi[:], xi[:], row("mm_lb"), ALU.add))
                dve.sem_inc(xi_ready, 1)

            def head_target(pair, par):
                dve.wait_ge(img_ready, 1).then_inc(img_ready, -1)
                dve.wait_ge(feat_landed[par], (pair + 1) * (3 * DMA))
                done(v.tensor_tensor(tgt[:], S[:, par, 2, :], S[:, par, 3, :], ALU.add))
                dve.sem_inc(tgt_ready, 1)

            def head_tT(par):
                dve.wait_ge(m_ready, 1).then_inc(m_ready, -1)
                done(v.tensor_copy(tT[:, par, :], mps[:, 0:P]))
                dve.sem_inc(tT_ready, 1)

            def head_T(par):
                dve.wait_ge(m_ready, 1).then_inc(m_ready, -1)
                done(v.tensor_tensor(Tt[:, par, :], mps[:, P:P + HID], row("ab1"), ALU.add))
                dve.sem_inc(m_free, 1)

            def tile_start():
                done(v.memset(rmax[:], LEAST))
                done(v.memset(rsum[:], 0.0))
                done(v.memset(acc[:], 0.0))

            def times_target(par):
                dve.wait_ge(eT_ready, 1).then_inc(eT_ready, -1)
                done(v.tensor_tensor(teT[:], eT[:], tT[:, par:par + 1, :].to_broadcast([P, SUB, P]), ALU.mult))
                dve.sem_inc(te_ready, 1)

            def scores(par, u):
                dve.wait_ge(h_ready, 1).then_inc(h_ready, -1)
                done(v.tensor_tensor(hid[:], hps[:, 0:SUB * HID].rearrange("p (s h) -> p s h", s=SUB),
                                     Tt[:, par:par + 1, :].to_broadcast([P, SUB, HID]), ALU.add))
                dve.sem_inc(h_free, 1)
                dve.sem_inc(eT_free, 1)
                done(v.scalar_tensor_tensor(out=hid[:], in0=hid[:], scalar=0.0,
                                            in1=row("aw2").rearrange("p (o h) -> p o h", o=1).to_broadcast([P, SUB, HID]),
                                            op0=ALU.max, op1=ALU.mult))
                done(v.tensor_reduce(sc[:, u * SUB:(u + 1) * SUB], hid[:], AX.X, ALU.add))

            def softmax_max(par, g):
                k = slice(g * GRP, (g + 1) * GRP)
                done(v.scalar_tensor_tensor(out=sc[:], in0=sc[:], scalar=row("ab2"), in1=keep[:, par, k],
                                            op0=ALU.add, op1=ALU.mult))
                done(v.tensor_tensor(sc[:], sc[:], mbias[:, par, k], ALU.add))
                done(v.tensor_reduce(gmax[:], sc[:], AX.X, ALU.max))
                done(v.tensor_scalar(nmax[:], gmax[:], rmax[:], -1.0, ALU.max, ALU.mult))
                dve.sem_inc(sc_ready, 1)

            def softmax_sum():
                dve.wait_ge(p_ready, 1).then_inc(p_ready, -1)
                done(v.scalar_tensor_tensor(out=rsum[:], in0=rsum[:], scalar=corr[:], in1=gsum[:],
                                            op0=ALU.mult, op1=ALU.add))
                done(v.tensor_scalar(rmax[:], nmax[:], -1.0, None, ALU.mult))

            def history(g):
                dve.wait_ge(pe_ready, 1).then_inc(pe_ready, -1)
                a = g * GRP
                done(v.tensor_tensor(e[:, a:a + 5, :], e[:, a:a + 5, :], e[:, a + 5:a + 10, :], ALU.add))
                done(v.tensor_tensor(e[:, a:a + 2, :], e[:, a:a + 2, :], e[:, a + 2:a + 4, :], ALU.add))
                done(v.tensor_tensor(e[:, a, :], e[:, a, :], e[:, a + 1, :], ALU.add))
                done(v.tensor_tensor(e[:, a, :], e[:, a, :], e[:, a + 4, :], ALU.add))
                done(v.scalar_tensor_tensor(out=acc[:], in0=acc[:], scalar=corr[:], in1=e[:, a, :],
                                            op0=ALU.mult, op1=ALU.add))
                dve.sem_inc(e_free, 1)

            def tail_history(par):
                done(v.reciprocal(rinv[:], rsum[:]))
                done(v.tensor_scalar(S[:, par, 4, :], acc[:], rinv[:], None, ALU.mult))

            def tail_gate_logits(par):
                done(v.tensor_reduce(z5[:], S[:, par, :, :], AX.X, ALU.add))
                w1v = row("se_w1").rearrange("p (j f) -> p j f", j=2)
                done(v.scalar_tensor_tensor(out=se10[:].rearrange("p (j f) -> p j f", j=2),
                                            in0=z5[:].rearrange("p (o f) -> p o f", o=1).to_broadcast([P, 2, FIELDS]),
                                            scalar=1.0 / EMB, in1=w1v, op0=ALU.mult, op1=ALU.mult))
                done(v.tensor_reduce(se2[:], se10[:].rearrange("p (j f) -> p j f", j=2), AX.X, ALU.add))
                done(v.tensor_tensor(se2[:], se2[:], row("se_b1"), ALU.add))
                done(v.tensor_scalar(se2[:], se2[:], 0.0, None, ALU.max))
                w2v = row("se_w2").rearrange("p (f j) -> p f j", j=2)
                done(v.tensor_tensor(se10[:].rearrange("p (f j) -> p f j", j=2),
                                     se2[:].rearrange("p (o j) -> p o j", o=1).to_broadcast([P, FIELDS, 2]), w2v, ALU.mult))
                done(v.tensor_reduce(g5[:], se10[:].rearrange("p (f j) -> p f j", j=2), AX.X, ALU.add))
                done(v.tensor_tensor(g5[:], g5[:], row("se_b2"), ALU.add))
                dve.sem_inc(gate_ready, 1)

            def tail_gate_apply(par):
                dve.wait_ge(gexp_ready, 1).then_inc(gexp_ready, -1)
                done(v.tensor_scalar(g5[:], g5[:], 1.0, None, ALU.add))
                done(v.reciprocal(g5[:], g5[:]))
                done(v.tensor_tensor(S[:, par, :, :], S[:, par, :, :],
                                     g5[:].rearrange("p (f o) -> p f o", o=1).to_broadcast([P, FIELDS, EMB]), ALU.mult))
                dve.sem_inc(se_ready, 1)

            def tail_pairs():
                dve.wait_ge(m_ready, 1).then_inc(m_ready, -1)
                at = FIELDS
                for i in range(4):
                    n = FIELDS - 1 - i
                    done(v.tensor_tensor(dn[:, at:at + n, :], dn[:, i + 1:FIELDS, :],
                                         mps[:, i * P:(i + 1) * P].rearrange("p (o b) -> p o b", o=1).to_broadcast([P, n, P]),
                                         ALU.mult))
                    at += n
                dve.sem_inc(m_free, 1)
                dve.sem_inc(dn_full, 1)

            def w_lo(raw_slot, slot, n=KG * P):
                dve.wait_ge(hi_done, 1).then_inc(hi_done, -1)
                done(v.tensor_tensor(Wl[:, slot, 0:n], raw[:, raw_slot, 0:n], Wh[:, slot, 0:n].bitcast(F32), ALU.subtract))
                dve.sem_inc(w_ready, 1)
                dve.sem_inc(raw_free, 1)

            def r_lo(raw_slot, k):
                dve.wait_ge(hi_done, 1).then_inc(hi_done, -1)
                done(v.tensor_tensor(X0l[:, k, :], raw[:, raw_slot, 0:NB], X0h[:, k, :].bitcast(F32), ALU.subtract))
                dve.sem_inc(x_ready, 1)
                dve.sem_inc(raw_free, 1)

            def x_new(layer, n):
                done(v.tensor_tensor(xnew[:], X0h[:, n, :].bitcast(F32), X0l[:, n, :].bitcast(F32), ALU.add))
                dve.wait_ge(mm_done, 1).then_inc(mm_done, -1)
                a, _ = COLS["cb"]
                bias = cols[:, bass.ds(n + (a + layer * FEATS), 1)]
                done(v.scalar_tensor_tensor(out=xnew[:], in0=xps[:, n % BANKS, :], scalar=bias, in1=xnew[:],
                                            op0=ALU.add, op1=ALU.mult))
                dve.sem_inc(bank_free, 1)
                if layer == 1:
                    done(v.tensor_tensor(xnew[:], xnew[:], X1h[:, n, :].bitcast(F32), ALU.add))
                    done(v.tensor_tensor(xnew[:], xnew[:], X1l[:, n, :].bitcast(F32), ALU.add))
                dve.sem_inc(xnew_ready, 1)

            def x_lo(layer, n):
                Xh, Xl = (X1h, X1l) if layer == 0 else (X0h, X0l)
                dve.wait_ge(xhi_done, 1).then_inc(xhi_done, -1)
                done(v.tensor_tensor(Xl[:, n, :], xnew[:], Xh[:, n, :].bitcast(F32), ALU.subtract))
                dve.sem_inc(x_ready, 1)

            def unit(q, last_layer):
                w_lo(w_slot(q), (q + 2) % RING, H1 if last_layer and q > 0 else KG * P)

            def fc_norm(j):
                x = h1[:, j, :]
                done(v.bn_stats(fstats[:], x))
                done(v.bn_aggr(fmv[:], fstats[:]))
                dve.sem_inc(fvar_ready, 1)
                dve.wait_ge(fsd_ready, 1).then_inc(fsd_ready, -1)
                done(v.reciprocal(frstd[:], fsd[:]))
                done(v.tensor_scalar(h1n[:], x, fmv[:, 0:1], frstd[:], ALU.subtract, ALU.mult))
                dve.sem_inc(h1n_ready, 1)

            def fc_norm2():
                dve.wait_ge(fmm_ready, 1).then_inc(fmm_ready, -1)
                done(v.tensor_tensor(h2, xps[:, FCB, 0:H2], row("b2"), ALU.add))
                dve.sem_inc(fc_free, 1)
                done(v.bn_stats(fstats[:], h2))
                done(v.bn_aggr(fmv[:], fstats[:]))
                dve.sem_inc(fvar_ready, 1)
                dve.wait_ge(fsd_ready, 1).then_inc(fsd_ready, -1)
                done(v.reciprocal(frstd[:], fsd[:]))
                done(v.tensor_scalar(h2, h2, fmv[:, 0:1], frstd[:], ALU.subtract, ALU.mult))
                dve.sem_inc(h2n_ready, 1)

            def fc_logit(at):
                dve.wait_ge(fmm_ready, 1).then_inc(fmm_ready, -1)
                done(v.tensor_tensor(logits[:, bass.ds(at, 1)], xps[:, FCB, 0:1], row("b3"), ALU.add))
                dve.sem_inc(fc_free, 1)

            def fc_step(c, n, first):
                if first:
                    r_lo(R14_SLOT, FEATS - 1)
                else:
                    fc_logit(c * TPC + n - 1)
                fc_norm(n)
                if not first:
                    x_new(0, n - 1)
                unit(0, False)
                if not first:
                    x_lo(0, n - 1)
                unit(1, False)
                unit(2, False)
                fc_norm2()

            def plain_step(layer, n, pending, last=False):
                m = n - 1 if pending == layer else FEATS - 1
                x_new(pending, m)
                unit(0, False)
                x_lo(pending, m)
                unit(1, last)
                unit(2, last)

            def w1_stage(more):
                for k in range(FEATS):
                    ws, rs = w1_slots(k, more)
                    if k == 0:
                        x_new(1, FEATS - 1)
                    if k + 2 < FEATS:
                        w_lo(ws, (k + 2) % RING, H1)
                    elif more:
                        w_lo(ws, (k + 2) % RING)
                    if k == 0:
                        x_lo(1, FEATS - 1)
                    if more and k:
                        r_lo(rs, k - 1)
                dve.wait_ge(mm_done, 1).then_inc(mm_done, -1)
                for b in range(TPC):
                    done(v.tensor_tensor(h1[:, b, :], xps[:, b, :], row("b1"), ALU.add))
                    dve.sem_inc(bank_free if b < BANKS else fc_free, 1)

            def chunk(c, more):
                fc_step(c, 0, True)
                with dve.Fori(1, TPC) as n:
                    fc_step(c, n, False)
                n = TPC
                fc_logit(c * TPC + n - 1)
                if more:
                    head_mask(0, (c + 1) * TPC)
                    head_var()
                x_new(0, n - 1)
                unit(0, False)
                x_lo(0, n - 1)
                if more:
                    head_norm()
                unit(1, False)
                if more:
                    head_target((c + 1) * (TPC // 2), 0)
                    head_tT(0)
                unit(2, False)
                if more:
                    head_T(0)
                    pending = None
                    for layer, third, grp, tail, head in SEGMENTS:
                        for i in range(5):
                            n = 5 * third + i
                            prev = (layer, n - 1) if n else (0, FEATS - 1)
                            last = layer == 1 and n == FEATS - 1
                            if grp is not None:
                                times_target(grp % 2)
                            x_new(*prev)
                            unit(0, False)
                            x_lo(*prev)
                            if pending is not None:
                                history(pending)
                                pending = None
                            if tail is not None and i == 0:
                                tail_history(tail % 2)
                            if grp is not None and i == 0:
                                tile_start()
                            if tail is not None and i == 1:
                                tail_pairs()
                            if head is not None and i == 1:
                                head_norm()
                            if grp is not None:
                                scores(grp % 2, 0)
                                times_target(grp % 2)
                            if tail is not None and i == 0:
                                tail_gate_logits(tail % 2)
                            unit(1, last)
                            if tail is not None and i == 0:
                                tail_gate_apply(tail % 2)
                            if head is not None and i == 1:
                                head_target((c + 1) * (TPC // 2) + head // 2, head % 2)
                            if grp is not None:
                                scores(grp % 2, 1)
                                softmax_max(grp % 2, i)
                            unit(2, last)
                            if head is not None and i == 0:
                                head_mask(head % 2, (c + 1) * TPC + head)
                                head_var()
                                if head == TPC - 1:
                                    dve.sem_inc(emb_free, 1)
                            if head is not None and i == 1:
                                head_tT(head % 2)
                            if grp is not None:
                                softmax_sum()
                                pending = i
                            if head is not None and i == 1:
                                head_T(head % 2)
                else:
                    with dve.Fori(TPC + 1, FEATS) as n:
                        plain_step(0, n, 0)
                    plain_step(1, 0, 0)
                    with dve.Fori(1, FEATS - 1) as n:
                        plain_step(1, n, 1)
                    plain_step(1, FEATS - 1, 1, True)
                w1_stage(more)

            dve.sem_inc(emb_free, 1)
            dve.sem_inc(raw_free, RING)
            dve.sem_inc(bank_free, BANKS)
            dve.sem_inc(fc_free, 1)
            dve.sem_inc(e_free, NG)
            dve.sem_inc(eT_free, 1)
            dve.sem_inc(h_free, 1)
            dve.sem_inc(m_free, 1)
            done(v.memset(eps[:], EPS))
            dve.wait_ge(consts_in, NCONST * DMA)
            done(v.tensor_tensor(A02[:], aw1[:, 0, :], aw1[:, 2, :], ALU.add))
            done(v.tensor_tensor(A12[:], aw1[:, 1, :], aw1[:, 2, :], ALU.subtract))
            done(v.tensor_scalar(col("cb", 0, FEATS), col("cb", 0, FEATS), 1.0, None, ALU.add))
            dve.sem_inc(consts_ok, 2)
            for u in range(2):
                w_lo(u, u)
            dve.wait_ge(idx_in, DMA)
            dve.wait_ge(emb_landed, DMA)
            with dve.Fori(0, TPC // 2) as i:
                for par in range(2):
                    t = i * 2 + par
                    head_mask(par, t)
                    done(v.tensor_copy(tgt[:], emb4[:, bass.ds(t * P, P)]))
                    dve.sem_inc(tgt_ready, 1)
                    head_var()
                    head_norm()
                    head_target(i, par)
                    head_tT(par)
                    head_T(par)
                    tile_start()
                    for g in range(NG):
                        for u in range(2):
                            times_target(par)
                            scores(par, u)
                        softmax_max(par, g)
                        softmax_sum()
                        history(g)
                    tail_history(par)
                    tail_gate_logits(par)
                    tail_gate_apply(par)
                    tail_pairs()
            dve.wait_ge(emb_landed, DMA).then_inc(emb_landed, -DMA)
            dve.sem_inc(emb_free, 1)
            for k in range(FEATS - 1):
                r_lo((2 + k) % RING, k)
            done(v.memset(h1, 0.0))
            with dve.Fori(0, nchunks - 1) as c:
                chunk(c, True)
            chunk(nchunks - 1, False)
            for j in range(TPC):
                fc_norm(j)
                fc_norm2()
                fc_logit(nchunks * TPC + j)
            dve.sem_inc(logits_ready, 1)
            dve.wait_ge(lexp_ready, 1).then_inc(lexp_ready, -1)
            done(v.tensor_scalar(probs[:], probs[:], 1.0, None, ALU.add))
            done(v.reciprocal(probs[:], probs[:]))
            dve.sem_inc(probs_ready, 1)
            dve.wait_ge(probsT_ready, 1).then_inc(probsT_ready, -1)
            done(v.tensor_copy(res[:], xps[0:ntiles, FCB, 0:P]))
            dve.sem_inc(res_ready, 1)


def kernel(**inputs):
    import numpy as np
    import concourse.bacc as bacc
    from concourse.bass_utils import run_bass_kernel_spmd as run

    x = {k.removeprefix("L0_rec_"): np.asarray(a) for k, a in inputs.items()}
    batch = x["r_item_seq"].shape[0]
    tiles = batch // P

    def column(name):
        return x[name].reshape(-1, 1)

    idx = np.concatenate([x["r_item_seq"], column("r_item_id"), column("r_likes_level"), column("r_views_level")], axis=1)
    rows = {"mm_b": x["mm_b"], "mm_g": x["mm_ln_g"], "mm_lb": x["mm_ln_b"], "ab1": x["ab1"], "aw2": x["aw2"], "b1": x["b1"],
            "b2": x["b2"], "se_w1": x["se_w1"].T, "se_b1": x["se_b1"], "se_w2": x["se_w2"].T, "se_b2": x["se_b2"],
            "ab2": x["ab2"], "b3": x["b3"]}
    cols = {"g1": x["ln1g"], "lb1": x["ln1b"], "g2": x["ln2g"], "lb2": x["ln2b"], "w3": x["w3"], "cb": x["cross_bias"]}
    host = {
        "idx": idx.reshape(tiles, P, SEQ + 3).transpose(1, 0, 2),
        "item_table": x["item_table"],
        "cate_table": x["cate_table"],
        "embT": x["r_item_emb_d128"].T,
        "rows": np.broadcast_to(np.concatenate([rows[k].reshape(-1) for k in ROWS]), (P, NROWS)),
        "cols": np.concatenate([cols[k].reshape(-1, P).T for k in COLS], axis=1),
        "mm_w": x["mm_w"],
        "aw1": x["aw1"],
        "bil_W": x["bil_W"],
        "cross_K": x["cross_K"].reshape(2, UNITS, KG, P, FEATS, P).transpose(0, 4, 1, 3, 2, 5)
                   .reshape(2 * FEATS * UNITS, P, KG * P),
        "w1": x["w1"],
        "w2": x["w2"],
    }
    nc = bacc.Bacc("TRN2", target_bir_lowering=False, num_devices=1, dynamic_dma_scratch_size=8192)
    arrays, args = {}, []
    for name, a in host.items():
        a = np.ascontiguousarray(a)
        arrays[f"in_{name}"] = a
        args.append(nc.dram_tensor(f"in_{name}", a.shape, mybir.dt.from_np(a.dtype), kind="ExternalInput").ap())
    out = nc.dram_tensor("out_probs", (tiles, P), F32, kind="ExternalOutput").ap()
    build(nc, *args, out, tiles)
    r = run(nc, [arrays], core_ids=[0])
    return r.results[0]["out_probs"].reshape(batch)
```

```python
from contextlib import ExitStack

import concourse.bass as bass
from concourse import mybir

ALU = mybir.AluOpType
ACT = mybir.ActivationFunctionType
AX = mybir.AxisListType
F32 = mybir.dt.float32
F32R = mybir.dt.float32r
I32 = mybir.dt.int32

P = 128
EMB = 128
SEQ = 50
HID = 64
FIELDS = 5
FEATS = FIELDS + FIELDS * (FIELDS - 1) // 2
TPC = 4
NB = TPC * P
GRP = 10
SUB = 5
NG = SEQ // GRP
KG = 5
UNITS = FEATS // KG
H1 = 512
H2 = 256
RING = 3
BANKS = 3
EPS = 1e-5
LEAST = -3.0e38
MASKED = -1.0e9
DMA = 16

ROWS = {}
_at = 0
for _name, _n in (("mm_b", EMB), ("mm_g", EMB), ("mm_lb", EMB), ("b1", H1),
                  ("b2", H2), ("se_w1", 2 * FIELDS), ("se_b1", 2), ("se_w2", 2 * FIELDS), ("se_b2", FIELDS),
                  ("ab2", 1), ("b3", 1)):
    ROWS[_name] = (_at, _at + _n)
    _at += _n
NROWS = _at
COLS = {}
_at = 0
for _name, _n in (("g1", 4), ("lb1", 4), ("g2", 2), ("lb2", 2), ("w3", 2), ("cb", 2 * FEATS), ("ab1", 1), ("aw2", 1)):
    COLS[_name] = (_at, _at + _n)
    _at += _n
NCOLS = _at

FC_STEPS = 6
SEGMENTS = [(0, 0, None, None, 0), (0, 1, 0, None, 1), (0, 2, 1, 0, 2), (1, 0, 2, 1, 3), (1, 1, 3, 2, None),
            (1, 2, None, 3, None)]


class Step:

    def __init__(self, layer, n, grp, g, follows, opened, tail, head, head_before, fc):
        self.layer, self.n, self.grp, self.g, self.follows, self.open = layer, n, grp, g, follows, opened
        self.tail, self.head, self.fc = tail, head, fc
        self.i = n % 5
        self.head_before = head_before


def steps():
    plan = []
    for at, (layer, fifth, grp, tail, head) in enumerate(SEGMENTS):
        for i in range(5):
            after = SEGMENTS[at + (i == 4)][2] if at + (i == 4) < len(SEGMENTS) else None
            before = SEGMENTS[at - (i == 0)][2] if at - (i == 0) >= 0 else None
            plan.append(Step(layer, 5 * fifth + i, grp, i, None if after is None else (after, (i + 1) % 5),
                             None if before is None else (before, (i - 1) % 5), tail, head, SEGMENTS[at - 1][4] if at and i == 0 else None,
                             layer == 0 and 5 * fifth + i < FC_STEPS))
    return plan


def link(eng, sem, ins):
    ins.then_inc(sem, 1)
    eng.wait_ge(sem, 1).then_inc(sem, -1)


def build(nc, idx_d, table_d, cate_d, embT_d, rows_d, cols_d, mmw_d, aw1_d, bil_d, kx_d, w1_d, w2_d, out_d, ntiles):
    nchunks = ntiles // TPC
    with ExitStack() as ctx:
        def sb(name, shape, dt=F32):
            return ctx.enter_context(nc.sbuf_tensor(name, shape, dt))

        def ps(name, shape):
            return ctx.enter_context(nc.psum_tensor(name, shape, F32))

        def sem(name):
            return ctx.enter_context(nc.semaphore(name))

        dnn_d = nc.dram_tensor("dnn_scratch", (nchunks, FEATS, P, TPC, P), F32, kind="Internal").ap()

        xps = ps("xps", [P, BANKS + 1, 512])
        FCB = BANKS
        mps = xps[:, FCB, :]
        aps = ps("aps", [P, 2 * 512])
        tps = aps[:, 0:SUB * P]
        hps = ps("hps", [P, 2 * 512])
        SCORES = SUB * P

        X0h = sb("X0h", [P, FEATS, NB], F32R)
        X0l = sb("X0l", [P, FEATS, NB], F32R)
        X1h = sb("X1h", [P, FEATS, NB], F32R)
        X1l = sb("X1l", [P, FEATS, NB], F32R)
        raw = sb("raw", [P, RING, KG * P])
        Wh = sb("Wh", [P, RING, KG * P], F32R)
        Wl = sb("Wl", [P, RING, KG * P], F32R)
        xnew = sb("xnew", [P, NB])
        e = sb("e", [P, NG * GRP, EMB])
        eT = sb("eT", [P, SUB * P])
        teT = sb("teT", [P, SUB * P])
        xsum = sb("xsum", [P, NB])
        idx_all = sb("idx_all", [P, ntiles, SEQ + 3], I32)
        idx_cur = sb("idx_cur", [P, 2, SEQ + 3], I32)
        S = sb("S", [P, 2, FIELDS, EMB])
        tT = sb("tT", [P, 2, P])
        Tt = sb("Tt", [HID, 2, P])
        keep = sb("keep", [P, 2, SEQ])
        mbias = sb("mbias", [P, 2, SEQ])
        hid = sb("hid", [HID, SUB * P])
        sc = sb("sc", [P, GRP])
        pw = sb("pw", [P, GRP])
        gmax = sb("gmax", [P, 1])
        nmax = sb("nmax", [P, NG])
        corr = sb("corr", [P, NG])
        gsum = sb("gsum", [P, NG])
        rsum = sb("rsum", [P, NG])
        sd = sb("sd", [P, 1])
        rinv = sb("rinv", [P, 1])
        acc = sb("acc", [P, 2, EMB])
        emb = sb("emb", [P, P])
        xi = sb("xi", [P, EMB])
        tgt = sb("tgt", [P, EMB])
        stats = sb("stats", [P, 6])
        mv = sb("mv", [P, 2])
        rstd = sb("rstd", [P, 1])
        fstats = sb("fstats", [P, 6])
        fmv = sb("fmv", [P, TPC, 2])
        fsd = sb("fsd", [P, TPC])
        frstd = sb("frstd", [P, TPC])
        z5 = sb("z5", [P, FIELDS])
        se10 = sb("se10", [P, 2 * FIELDS])
        se2 = sb("se2", [P, 2])
        g5 = sb("g5", [P, FIELDS])
        dn = sb("dn", [P, TPC * H1 // P, P])
        h1 = dn[:].rearrange("p f b -> p (f b)").rearrange("p (t n) -> p t n", t=TPC)

        def h1_T(j):
            return h1[:, j, :].rearrange("p (k b) -> p k b", b=P)


        def h2(j):
            return h1[:, j, 0:H2]

        def g2T(pair, k):
            return h1[:, 2 * pair:2 * pair + 2, H2 + k * P:H2 + (k + 1) * P]

        logits = sb("logits", [P, TPC * (nchunks + 1)])
        probs = sb("probs", [P, ntiles])
        ident = sb("ident", [P, P])
        eps = sb("eps", [P, 1])
        rows = sb("rows", [P, NROWS])
        cols = sb("cols", [P, NCOLS])
        mmw = sb("mmw", [P, EMB])
        A3 = sb("A3", [P, HID])
        A02 = sb("A02", [P, HID])
        A12 = sb("A12", [P, HID])
        bil = sb("bil", [P, 4, EMB])
        w2 = sb("w2", [P, H1 // P, H2])

        aw1 = xsum[:, 0:4 * HID].rearrange("p (q n) -> p q n", q=4)

        def row(name):
            a, b = ROWS[name]
            return rows[:, a:b]

        def col(name, k, n=1):
            a, _ = COLS[name]
            return cols[:, a + k:a + k + n]

        consts_in = sem("consts_in")
        consts_ok = sem("consts_ok")
        ident_ok = sem("ident_ok")
        ident_z = sem("ident_z")
        idx_in = sem("idx_in")
        act_done = sem("act_done")
        dve_done = sem("dve_done")
        pool_done = sem("pool_done")
        raw_landed = [sem(f"raw_landed{i}") for i in range(RING)]
        raw_free = sem("raw_free")
        split_free = sem("split_free")
        hi_done = sem("hi_done")
        w_ready = sem("w_ready")
        x_ready = sem("x_ready")
        x0_free = sem("x0_free")
        bank_free = sem("bank_free")
        mm_done = sem("mm_done")
        xnew_ready = sem("xnew_ready")
        xhi_done = sem("xhi_done")
        emb_landed = sem("emb_landed")
        dnn_stored = sem("dnn_stored")
        dnn_ready = sem("dnn_ready")
        feat_landed = [sem(f"feat_landed{i}") for i in range(2)]
        e_landed = [sem(f"e_landed{i}") for i in range(NG)]
        S_free = sem("S_free")
        tp_ready = sem("tp_ready")
        tp_free = sem("tp_free")
        eT_ready = sem("eT_ready")
        eT_free = sem("eT_free")
        te_ready = sem("te_ready")
        h_ready = sem("h_ready")
        hid_added = sem("hid_added")
        hid_ready = sem("hid_ready")
        scores_read = sem("scores_read")
        dots_ready = sem("dots_ready")
        sc_ready = sem("sc_ready")
        p_ready = sem("p_ready")
        weighed = sem("weighed")
        acc_scaled = sem("acc_scaled")
        acc_ready = sem("acc_ready")
        lo_done = sem("lo_done")
        bank4_free = sem("bank4_free")
        m_ready = sem("m_ready")
        xi_ready = sem("xi_ready")
        var_ready = sem("var_ready")
        sd_ready = sem("sd_ready")
        fvar_ready = sem("fvar_ready")
        fsd_ready = sem("fsd_ready")
        img_ready = sem("img_ready")
        tgt_ready = sem("tgt_ready")
        tT_ready = sem("tT_ready")
        gate_ready = sem("gate_ready")
        gexp_ready = sem("gexp_ready")
        se_ready = sem("se_ready")
        seT_ready = sem("seT_ready")
        dn_full = sem("dn_full")
        h1n_ready = sem("h1n_ready")
        fT_ready = sem("fT_ready")
        g_ready = sem("g_ready")
        fmm_ready = sem("fmm_ready")
        h2n_ready = sem("h2n_ready")
        logits_ready = sem("logits_ready")
        lexp_ready = sem("lexp_ready")
        probs_ready = sem("probs_ready")
        probsT_ready = sem("probsT_ready")
        res_ready = sem("res_ready")
        out_stored = sem("out_stored")

        NCONST = 6
        AB1, AW2 = COLS["ab1"][0], COLS["aw2"][0]
        plan = steps()

        UL = FEATS * UNITS
        START = 2 + FEATS - 1
        R14_SLOT = START % RING

        def w_slot(q):
            return (q + 2) % RING

        def w1_slots(k, refill):
            at = START + 2 * UL + 1 + (2 * k - 1 if refill and k else k)
            return at % RING, (at + 1) % RING

        def e_sub(g, u, s):
            return e[:, g * GRP + u * SUB + s, :]

        block = ctx.enter_context(nc.Block())

        @block.sync
        def _(sp):
            def load(slot, src, n):
                sp.wait_ge(raw_free, 1).then_inc(raw_free, -1)
                sp.dma_start(raw[:, slot, 0:n], src).then_inc(raw_landed[slot], DMA)

            def k_unit(u, slot):
                load(slot, kx_d[u], KG * P)

            def w1_unit(k, slot):
                load(slot, w1_d[k * P:(k + 1) * P, :], H1)

            def r_unit(c, k, slot):
                load(slot, dnn_d[c, k].rearrange("p t b -> p (t b)"), NB)

            sp.dma_start(idx_all[:], idx_d).then_inc(idx_in, DMA)
            sp.dma_start(mmw[:], mmw_d).then_inc(consts_in, DMA)
            sp.dma_start(rows[:], rows_d).then_inc(consts_in, DMA)
            sp.dma_start(cols[:], cols_d).then_inc(consts_in, DMA)
            sp.dma_start(aw1, aw1_d.rearrange("(q p) n -> p q n", p=P)).then_inc(consts_in, DMA)
            sp.dma_start(bil[:], bil_d.rearrange("i d e -> d i e")).then_inc(consts_in, DMA)
            sp.dma_start(w2[:], w2_d.rearrange("(k p) n -> p k n", p=P)).then_inc(consts_in, DMA)
            k_unit(0, 0)
            k_unit(1, 1)
            sp.wait_ge(dnn_ready, TPC).then_inc(dnn_ready, -TPC)
            for k in range(FEATS - 1):
                r_unit(0, k, (2 + k) % RING)

            def chunk(c, more):
                r_unit(c, FEATS - 1, R14_SLOT)
                with sp.Fori(0, (2 * UL - 3) // RING) as i:
                    for j in range(RING):
                        k_unit(i * RING + 2 + j, (2 + j) % RING)
                k_unit(2 * UL - 1, (2 * UL - 1) % RING)
                w1_unit(0, w_slot(2 * UL - 2))
                w1_unit(1, w_slot(2 * UL - 1))
                for k in range(FEATS):
                    ws, rs = w1_slots(k, more)
                    if k + 2 < FEATS:
                        w1_unit(k + 2, ws)
                    elif more:
                        k_unit(k + 2 - FEATS, ws)
                    if more and k:
                        if k == 1:
                            sp.wait_ge(dnn_ready, TPC).then_inc(dnn_ready, -TPC)
                        r_unit(c + 1, k - 1, rs)

            with sp.Fori(0, nchunks - 1) as c:
                chunk(c, True)
            chunk(nchunks - 1, False)
            sp.wait_ge(res_ready, 1).then_inc(res_ready, -1)
            sp.dma_start(out_d, xi[0:ntiles, :]).then_inc(out_stored, DMA)
            sp.wait_ge(out_stored, DMA)

        @block.gpsimd
        def _(pool):
            nc.gpsimd.memset(ident[:], 0.0).then_inc(ident_z, 1)
            pool.wait_ge(ident_z, 1).then_inc(ident_z, -1)
            nc.gpsimd.affine_select(out=ident[:], in_=ident[:], compare_op=ALU.not_equal, fill=1.0, base=0,
                                    pattern=[[-1, P]], channel_multiplier=1).then_inc(ident_ok, 1)
            pool.wait_ge(idx_in, DMA)

            def gather(dst, table, par, s, landed):
                nc.gpsimd.indirect_dma_start(
                    out=dst, out_offset=None, in_=table,
                    in_offset=bass.IndirectOffsetOnAxis(ap=idx_cur[:, par, s:s + 1], axis=0),
                ).then_inc(landed, DMA)

            def indices(t, par):
                link(pool, pool_done, nc.gpsimd.tensor_copy(idx_cur[:, par, :], idx_all[:, t, :]))

            def features(par):
                pool.wait_ge(S_free, 1).then_inc(S_free, -1)
                gather(S[:, par, 2, :], table_d, par, SEQ, feat_landed[par])
                gather(S[:, par, 0, :], cate_d, par, SEQ + 1, feat_landed[par])
                gather(S[:, par, 1, :], cate_d, par, SEQ + 2, feat_landed[par])

            def embeddings(par, g):
                for s in range(GRP):
                    gather(e[:, g * GRP + s, :], table_d, par, g * GRP + s, e_landed[g])

            def history(par, g):
                a = g * GRP
                own = acc[:, par, :] if g == 0 else e[:, a, :]
                pool.wait_ge(weighed, 1).then_inc(weighed, -1)
                if g:
                    nc.gpsimd.tensor_scalar(acc[:, par, :], acc[:, par, :], corr[:, g:g + 1], None,
                                            ALU.mult).then_inc(acc_scaled, 1)
                link(pool, pool_done, nc.gpsimd.tensor_tensor(e[:, a:a + 5, :], e[:, a:a + 5, :], e[:, a + 5:a + 10, :], ALU.add))
                link(pool, pool_done, nc.gpsimd.tensor_tensor(e[:, a:a + 2, :], e[:, a:a + 2, :], e[:, a + 2:a + 4, :], ALU.add))
                link(pool, pool_done, nc.gpsimd.tensor_tensor(e[:, a, :], e[:, a, :], e[:, a + 1, :], ALU.add))
                link(pool, pool_done, nc.gpsimd.tensor_tensor(own, e[:, a, :], e[:, a + 4, :], ALU.add))
                if g:
                    pool.wait_ge(acc_scaled, 1).then_inc(acc_scaled, -1)
                    link(pool, pool_done, nc.gpsimd.tensor_tensor(acc[:, par, :], acc[:, par, :], e[:, a, :], ALU.add))
                if g == NG - 1:
                    pool.sem_inc(acc_ready, 1)

            def tile(t, par, more):
                if more:
                    indices(t + 1, 1 - par)
                for g in range(NG):
                    history(par, g)
                    if more:
                        if g == 2:
                            features(1 - par)
                        embeddings(1 - par, g)

            indices(0, 0)
            features(0)
            for g in range(NG):
                embeddings(0, g)
            with pool.Fori(0, ntiles // 2 - 1) as i:
                for par in range(2):
                    tile(i * 2 + par, par, True)
            tile(ntiles - 2, 0, True)
            tile(ntiles - 1, 1, False)

        @block.tensor
        def _(pe):
            mm = nc.tensor.matmul

            def transposes(t, g, u):
                if u == 0:
                    pe.wait_ge(e_landed[g], (t + 1) * (DMA * GRP))
                pe.wait_ge(tp_free, 1).then_inc(tp_free, -1)
                for s in range(SUB):
                    last = nc.tensor.transpose(tps[:, s * P:(s + 1) * P], e_sub(g, u, s), ident[:])
                last.then_inc(tp_ready, 1)

            def hidden(u):
                if u == 0:
                    pe.wait_ge(scores_read, 1).then_inc(scores_read, -1)
                pe.wait_ge(te_ready, 1).then_inc(te_ready, -1)
                near, far = slice(0, 512), slice(512, SUB * P)
                mm(hps[0:HID, near], A12[:], eT[:, near], start=True, stop=False)
                mm(hps[0:HID, far], A12[:], eT[:, far], start=True, stop=False).then_inc(eT_free, 1)
                mm(hps[0:HID, near], A3[:], teT[:, near], start=False, stop=True)
                last = mm(hps[0:HID, far], A3[:], teT[:, far], start=False, stop=True)
                last.then_inc(h_ready, 1)

            def dots(u):
                pe.wait_ge(hid_ready, 1).then_inc(hid_ready, -1)
                for s in range(SUB):
                    at = SCORES + u * SUB + s
                    last = mm(hps[:, at:at + 1], hid[:, s * P:(s + 1) * P], cols[0:HID, AW2:AW2 + 1], start=True, stop=True)
                if u:
                    last.then_inc(dots_ready, 1)

            def head_mm():
                pe.wait_ge(emb_landed, DMA).then_inc(emb_landed, -DMA)
                pe.wait_ge(bank4_free, 1).then_inc(bank4_free, -1)
                mm(mps[:, 0:P], emb[:], mmw[:], start=True, stop=True).then_inc(m_ready, 1)

            def head_turn():
                pe.wait_ge(tgt_ready, 1).then_inc(tgt_ready, -1)
                pe.wait_ge(bank4_free, 1).then_inc(bank4_free, -1)
                nc.tensor.transpose(mps[:, 0:P], tgt[:], ident[:]).then_inc(m_ready, 1)

            def head_share(par):
                pe.wait_ge(tT_ready, 1).then_inc(tT_ready, -1)
                mm(mps[0:HID, P:2 * P], A02[:], tT[:, par, :], start=True, stop=True).then_inc(m_ready, 1)

            def tail_turn(par):
                pe.wait_ge(se_ready, 1).then_inc(se_ready, -1)
                pe.wait_ge(tp_free, 1).then_inc(tp_free, -1)
                for f in range(FIELDS):
                    last = nc.tensor.transpose(tps[:, f * P:(f + 1) * P], S[:, par, f, :], ident[:])
                last.then_inc(tp_ready, 1)

            def tail_bilinear():
                pe.wait_ge(seT_ready, 1).then_inc(seT_ready, -1)
                pe.wait_ge(bank4_free, 1).then_inc(bank4_free, -1)
                for i in range(4):
                    last = mm(mps[:, i * P:(i + 1) * P], bil[:, i, :], dn[:, i, :], start=True, stop=True)
                last.then_inc(m_ready, 1)

            def products(layer, n, kg, first):
                Xh, Xl = (X0h, X0l) if layer == 0 else (X1h, X1l)
                out = xps[:, n % BANKS, :]
                if kg == 0:
                    pe.wait_ge(bank_free, 1).then_inc(bank_free, -1)
                pe.wait_ge(w_ready, 1).then_inc(w_ready, -1)
                for i in range(KG):
                    k = kg * KG + i
                    if first:
                        pe.wait_ge(x_ready, 1).then_inc(x_ready, -1)
                    wh, wl = Wh[:, kg, i * P:(i + 1) * P], Wl[:, kg, i * P:(i + 1) * P]
                    m0 = mm(out, wh, Xh[:, k, :], start=(k == 0), stop=False)
                    m1 = mm(out, wh, Xl[:, k, :], start=False, stop=False)
                    m2 = mm(out, wl, Xh[:, k, :], start=False, stop=(k == FEATS - 1))
                    if i == 0:
                        m0.then_inc(split_free, 1)
                        if layer == 0 and first and kg == 0:
                            m1.then_inc(x0_free, 1)
                if kg == UNITS - 1:
                    m2.then_inc(mm_done, 1)

            def w1_products(more):
                for k in range(FEATS):
                    pe.wait_ge(w_ready, 1).then_inc(w_ready, -1)
                    pe.wait_ge(x_ready, 1).then_inc(x_ready, -1)
                    s = k % RING
                    for b in (0, 1, 3, 2):
                        if k == 0 and b < BANKS:
                            pe.wait_ge(bank_free, 1).then_inc(bank_free, -1)
                        elif k == 0:
                            pe.wait_ge(bank4_free, 1).then_inc(bank4_free, -1)
                        out = xps[:, b, :]
                        xh, xl = X0h[:, k, b * P:(b + 1) * P], X0l[:, k, b * P:(b + 1) * P]
                        m0 = mm(out, xh, Wh[:, s, 0:H1], start=(k == 0), stop=False)
                        m1 = mm(out, xh, Wl[:, s, 0:H1], start=False, stop=False)
                        m2 = mm(out, xl, Wh[:, s, 0:H1], start=False, stop=(k == FEATS - 1))
                        if b == 0:
                            m0.then_inc(split_free, 1)
                            if more and k:
                                m1.then_inc(x0_free, 1)
                m2.then_inc(mm_done, 1)

            def fc_turn1(j):
                pe.wait_ge(h1n_ready, 1).then_inc(h1n_ready, -1)
                pe.wait_ge(bank4_free, 1).then_inc(bank4_free, -1)
                for k in range(H1 // P):
                    last = nc.tensor.transpose(xps[:, FCB, k * P:(k + 1) * P], h1[:, j, k * P:(k + 1) * P], ident[:])
                last.then_inc(fT_ready, 1)

            def fc_w2(j):
                pe.wait_ge(g_ready, 1).then_inc(g_ready, -1)
                pe.wait_ge(bank4_free, 1).then_inc(bank4_free, -1)
                for k in range(H1 // P):
                    last = mm(xps[:, FCB, 0:H2], h1_T(j)[:, k, :], w2[:, k, :], start=(k == 0), stop=(k == H1 // P - 1))
                last.then_inc(fmm_ready, 1)

            def fc_turn2(pair):
                pe.wait_ge(h2n_ready, 1).then_inc(h2n_ready, -1)
                pe.wait_ge(bank4_free, 1).then_inc(bank4_free, -1)
                for k in range(H2 // P):
                    for i in range(2):
                        at = (2 * k + i) * P
                        last = nc.tensor.transpose(xps[:, FCB, at:at + P], h2(2 * pair + i)[:, k * P:(k + 1) * P], ident[:])
                last.then_inc(fT_ready, 1)

            def fc_w3():
                pe.wait_ge(g_ready, 2).then_inc(g_ready, -2)
                pe.wait_ge(bank4_free, 1).then_inc(bank4_free, -1)
                for j in range(TPC):
                    for k in range(H2 // P):
                        last = mm(mps[:, j:j + 1], g2T(j // 2, k)[:, j % 2, :], col("w3", k), start=(k == 0),
                                  stop=(k == H2 // P - 1))
                last.then_inc(fmm_ready, 1)

            def step(c, p, dense, more, fc=True):
                fc = fc and p.fc
                first = p.n == 0
                grp, tail, head = (p.grp, p.tail, p.head) if more else (None, None, None)
                if dense:
                    products(p.layer, p.n, 0, first)
                if grp is not None:
                    transposes((c + 1) * TPC + grp, p.g, 1)
                    hidden(0)
                if fc and p.n == 5:
                    fc_turn2(0)
                if head is not None and p.i == 2:
                    head_mm()
                if dense:
                    products(p.layer, p.n, 1, first)
                if grp is not None:
                    dots(0)
                    hidden(1)
                if tail is not None and p.i == 3:
                    tail_bilinear()
                if fc and p.n < TPC:
                    fc_turn1(p.n)
                if fc and p.n == 5:
                    fc_turn2(1)
                if more and p.follows is not None:
                    transposes((c + 1) * TPC + p.follows[0], p.follows[1], 0)
                if head is not None and p.i == 4:
                    head_turn()
                if dense:
                    products(p.layer, p.n, 2, first)
                if grp is not None:
                    dots(1)
                if tail is not None and p.i == 2:
                    tail_turn(tail % 2)
                if head is not None and p.i == 4:
                    head_share(head % 2)
                if fc and p.n < TPC:
                    fc_w2(p.n)
                if fc and p.n == 5:
                    fc_w3()

            def chunk(c, more):
                if more:
                    for p in plan:
                        step(c, p, True, True)
                else:
                    for p in plan[:FC_STEPS]:
                        step(c, p, True, False)
                    with pe.Fori(FC_STEPS, FEATS) as n:
                        for kg in range(UNITS):
                            products(0, n, kg, False)
                    for kg in range(UNITS):
                        products(1, 0, kg, True)
                    with pe.Fori(1, FEATS) as n:
                        for kg in range(UNITS):
                            products(1, n, kg, False)
                w1_products(more)

            pe.wait_ge(ident_ok, 1)
            pe.wait_ge(consts_ok, 1)
            for p in plan:
                step(-1, p, False, True, False)
            with pe.Fori(0, nchunks - 1) as c:
                chunk(c, True)
            chunk(nchunks - 1, False)
            for p in plan[:FC_STEPS]:
                step(nchunks, p, False, False)
            pe.wait_ge(probs_ready, 1).then_inc(probs_ready, -1)
            pe.wait_ge(bank4_free, 1).then_inc(bank4_free, -1)
            nc.tensor.transpose(xps[0:ntiles, FCB, 0:P], probs[:, :], ident[:]).then_inc(probsT_ready, 1)

        @block.scalar
        def _(act):
            af = nc.scalar.activation

            def done(ins):
                link(act, act_done, ins)

            def copy_eT():
                act.wait_ge(tp_ready, 1).then_inc(tp_ready, -1)
                act.wait_ge(eT_free, 1).then_inc(eT_free, -1)
                done(af(eT[:], tps, ACT.Copy))
                act.sem_inc(tp_free, 1)
                act.sem_inc(eT_ready, 1)

            def relu():
                act.wait_ge(hid_added, 1).then_inc(hid_added, -1)
                af(hid[:], hid[:], ACT.Relu).then_inc(hid_ready, 1)

            def exps(g):
                act.wait_ge(sc_ready, 1).then_inc(sc_ready, -1)
                if g:
                    af(corr[:, g:g + 1], nmax[:, g - 1:g], ACT.Exp, scale=-1.0, bias=nmax[:, g:g + 1])
                done(af(pw[:], sc[:], ACT.Exp, bias=nmax[:, g:g + 1], accum_out=gsum[:, g:g + 1]))
                act.sem_inc(p_ready, 1)

            def weigh(g):
                for s in range(GRP):
                    x = e[:, g * GRP + s, :]
                    last = af(x, x, ACT.Copy, scale=pw[:, s:s + 1])
                last.then_inc(weighed, 1)

            def head_load(t):
                act.dma_start(emb[:], embT_d[:, bass.ds(t * P, P)]).then_inc(emb_landed, DMA)

            def head_sd():
                act.wait_ge(var_ready, 1).then_inc(var_ready, -1)
                af(sd[:], mv[:, 1:2], ACT.Sqrt, bias=eps[:]).then_inc(sd_ready, 1)

            def head_gelu(par):
                act.wait_ge(xi_ready, 1).then_inc(xi_ready, -1)
                af(S[:, par, 3, :], xi[:], ACT.Gelu).then_inc(img_ready, 1)

            def tail_gate():
                act.wait_ge(gate_ready, 1).then_inc(gate_ready, -1)
                af(g5[:], g5[:], ACT.Exp, scale=-1.0).then_inc(gexp_ready, 1)

            def tail_copy():
                act.wait_ge(tp_ready, 1).then_inc(tp_ready, -1)
                done(af(dn[:, 0:FIELDS, :].rearrange("p s b -> p (s b)"), tps, ACT.Copy))
                act.sem_inc(tp_free, 1)
                act.sem_inc(S_free, 1)
                act.sem_inc(seT_ready, 1)

            def tail_store(c, j):
                act.wait_ge(dn_full, 1).then_inc(dn_full, -1)
                act.dma_start(dnn_d[c, :, :, j, :].rearrange("f p b -> p f b"), dn[:, 0:FEATS, :]).then_inc(dnn_stored, DMA)

            def tail_settle():
                act.wait_ge(dnn_stored, DMA).then_inc(dnn_stored, -DMA)
                act.sem_inc(dnn_ready, 1)

            def w_hi(raw_slot, slot, n=KG * P):
                act.wait_ge(raw_landed[raw_slot], DMA).then_inc(raw_landed[raw_slot], -DMA)
                act.wait_ge(split_free, 1).then_inc(split_free, -1)
                af(Wh[:, slot, 0:n], raw[:, raw_slot, 0:n], ACT.Copy).then_inc(hi_done, 1)

            def r_hi(raw_slot, k, reused=True):
                act.wait_ge(raw_landed[raw_slot], DMA).then_inc(raw_landed[raw_slot], -DMA)
                if reused:
                    act.wait_ge(x0_free, 1).then_inc(x0_free, -1)
                af(X0h[:, k, :], raw[:, raw_slot, 0:NB], ACT.Copy).then_inc(hi_done, 1)

            def x_hi(layer, n):
                act.wait_ge(xnew_ready, 1).then_inc(xnew_ready, -1)
                Xh = X1h if layer == 0 else X0h
                af(Xh[:, n, :], xnew[:], ACT.Copy).then_inc(xhi_done, 1)

            def fc_sd():
                act.wait_ge(fvar_ready, 1).then_inc(fvar_ready, -1)
                af(fsd[:], fmv[:, :, 1], ACT.Sqrt, bias=eps[:]).then_inc(fsd_ready, 1)

            def fc_gelu1(j):
                act.wait_ge(fT_ready, 1).then_inc(fT_ready, -1)
                for k in range(H1 // P):
                    last = af(h1_T(j)[:, k, :], xps[:, FCB, k * P:(k + 1) * P], ACT.Gelu, scale=col("g1", k), bias=col("lb1", k))
                done(last)
                act.sem_inc(bank4_free, 1)
                act.sem_inc(g_ready, 1)

            def fc_gelu2(pair):
                act.wait_ge(fT_ready, 1).then_inc(fT_ready, -1)
                for k in range(H2 // P):
                    last = af(g2T(pair, k), xps[:, FCB, 2 * k * P:2 * (k + 1) * P].rearrange("p (t b) -> p t b", t=2),
                              ACT.Gelu, scale=col("g2", k), bias=col("lb2", k))
                done(last)
                act.sem_inc(bank4_free, 1)
                act.sem_inc(g_ready, 1)

            def unit(q, last_layer):
                w_hi(w_slot(q), (q + 2) % RING, H1 if last_layer and q > 0 else KG * P)

            def step(c, p, dense, more, fc=True):
                fc = fc and p.fc
                grp, tail, head = (p.grp, p.tail, p.head) if more else (None, None, None)
                last = p.layer == 1 and p.n == FEATS - 1
                if head is not None and p.i == 0:
                    head_load((c + 1) * TPC + head)
                if dense:
                    if p.layer == 0 and p.n == 0:
                        r_hi(R14_SLOT, FEATS - 1)
                    unit(0, False)
                if more and p.open is not None:
                    exps(p.open[1])
                if dense and p.layer and p.n == 0:
                    x_hi(0, FEATS - 1)
                if more and p.open is not None:
                    weigh(p.open[1])
                if head is not None and p.i == 3:
                    head_gelu(head % 2)
                if tail is not None and p.i == 4:
                    tail_store(c + 1, tail)
                if grp is not None:
                    relu()
                    copy_eT()
                if dense:
                    unit(1, last)
                if fc and p.n in (0, 4):
                    fc_sd()
                if fc and p.n == 5:
                    fc_gelu2(0)
                if dense and p.n:
                    x_hi(p.layer, p.n - 1)
                if head is not None and p.i == 2:
                    head_sd()
                if tail is not None and p.i == 2:
                    tail_gate()
                if grp is not None:
                    relu()
                if more and p.follows is not None:
                    copy_eT()
                if fc and p.n < TPC:
                    fc_gelu1(p.n)
                if fc and p.n == 5:
                    fc_gelu2(1)
                if dense:
                    unit(2, last)
                if tail is not None and p.i == 2:
                    tail_copy()
                if tail is not None and p.i == 4:
                    tail_settle()

            def plain_step(layer, n, pending, last=False):
                unit(0, False)
                if pending is not None:
                    x_hi(pending, n - 1 if pending == layer else FEATS - 1)
                unit(1, last)
                unit(2, last)

            def w1_stage(more):
                for k in range(FEATS):
                    ws, rs = w1_slots(k, more)
                    if k + 2 < FEATS:
                        w_hi(ws, (k + 2) % RING, H1)
                    elif more:
                        w_hi(ws, (k + 2) % RING)
                    if k == 0:
                        x_hi(1, FEATS - 1)
                    if more and k:
                        r_hi(rs, k - 1)

            def chunk(c, more):
                if more:
                    for p in plan:
                        step(c, p, True, True)
                else:
                    for p in plan[:FC_STEPS]:
                        step(c, p, True, False)
                    with act.Fori(FC_STEPS, FEATS) as n:
                        plain_step(0, n, 0)
                    plain_step(1, 0, 0)
                    with act.Fori(1, FEATS - 1) as n:
                        plain_step(1, n, 1)
                    plain_step(1, FEATS - 1, 1, True)
                w1_stage(more)

            act.sem_inc(S_free, 2)
            act.sem_inc(tp_free, 1)
            act.sem_inc(eT_free, 1)
            act.wait_ge(consts_ok, 1).then_inc(consts_ok, -1)
            for u in range(2):
                act.wait_ge(raw_landed[u], DMA).then_inc(raw_landed[u], -DMA)
                af(Wh[:, u, :], raw[:, u, :], ACT.Copy).then_inc(hi_done, 1)
            for p in plan:
                step(-1, p, False, True, False)
            for k in range(FEATS - 1):
                r_hi((2 + k) % RING, k, False)
            with act.Fori(0, nchunks - 1) as c:
                chunk(c, True)
            chunk(nchunks - 1, False)
            for p in plan[:FC_STEPS]:
                step(nchunks, p, False, False)
            act.wait_ge(logits_ready, 1).then_inc(logits_ready, -1)
            af(probs[:], logits[:, TPC:TPC + ntiles], ACT.Exp, scale=-1.0).then_inc(lexp_ready, 1)

        @block.vector
        def _(dve):
            v = nc.vector

            def done(ins):
                link(dve, dve_done, ins)

            def head_mask(par, t):
                done(v.tensor_scalar(keep[:, par, :], idx_all[:, t, 0:SEQ], 0.0, None, ALU.not_equal))
                done(v.tensor_scalar(mbias[:, par, :], idx_all[:, t, 0:SEQ], 0.0, MASKED, ALU.is_equal, ALU.mult))

            def head_var():
                dve.wait_ge(m_ready, 1).then_inc(m_ready, -1)
                done(v.tensor_tensor(xi[:], mps[:, 0:P], row("mm_b"), ALU.add))
                dve.sem_inc(bank4_free, 1)
                done(v.bn_stats(stats[:], xi[:]))
                v.bn_aggr(mv[:], stats[:]).then_inc(var_ready, 1)

            def head_norm():
                dve.wait_ge(sd_ready, 1).then_inc(sd_ready, -1)
                done(v.reciprocal(rstd[:], sd[:]))
                done(v.tensor_scalar(xi[:], xi[:], mv[:, 0:1], rstd[:], ALU.subtract, ALU.mult))
                done(v.tensor_tensor(xi[:], xi[:], row("mm_g"), ALU.mult))
                v.tensor_tensor(xi[:], xi[:], row("mm_lb"), ALU.add).then_inc(xi_ready, 1)

            def head_target(pair, par):
                dve.wait_ge(img_ready, 1).then_inc(img_ready, -1)
                dve.wait_ge(feat_landed[par], (pair + 1) * (3 * DMA))
                done(v.tensor_tensor(tgt[:], S[:, par, 2, :], S[:, par, 3, :], ALU.add))
                dve.sem_inc(tgt_ready, 1)

            def head_tT(par):
                dve.wait_ge(m_ready, 1).then_inc(m_ready, -1)
                done(v.tensor_copy(tT[:, par, :], mps[:, 0:P]))
                dve.sem_inc(tT_ready, 1)

            def head_T(par):
                dve.wait_ge(m_ready, 1).then_inc(m_ready, -1)
                done(v.tensor_scalar(Tt[:, par, :], mps[0:HID, P:2 * P], cols[0:HID, AB1:AB1 + 1], None, ALU.add))
                dve.sem_inc(bank4_free, 1)

            def times_target(par):
                dve.wait_ge(eT_ready, 1).then_inc(eT_ready, -1)
                v.tensor_tensor(teT[:].rearrange("p (s b) -> p s b", s=SUB), eT[:].rearrange("p (s b) -> p s b", s=SUB),
                                tT[:, par:par + 1, :].to_broadcast([P, SUB, P]), ALU.mult).then_inc(te_ready, 1)

            def add_target(par):
                dve.wait_ge(h_ready, 1).then_inc(h_ready, -1)
                v.tensor_tensor(hid[:].rearrange("p (s b) -> p s b", s=SUB), hps[0:HID, 0:SUB * P].rearrange("p (s b) -> p s b", s=SUB),
                                Tt[:, par:par + 1, :].to_broadcast([HID, SUB, P]), ALU.add).then_inc(hid_added, 1)

            def softmax_max(par, g):
                k = slice(g * GRP, (g + 1) * GRP)
                dve.wait_ge(dots_ready, 1).then_inc(dots_ready, -1)
                done(v.scalar_tensor_tensor(out=sc[:], in0=hps[:, SCORES:SCORES + GRP], scalar=row("ab2"), in1=keep[:, par, k],
                                            op0=ALU.add, op1=ALU.mult))
                dve.sem_inc(scores_read, 1)
                done(v.tensor_tensor(sc[:], sc[:], mbias[:, par, k], ALU.add))
                done(v.tensor_reduce(gmax[:], sc[:], AX.X, ALU.max))
                before = nmax[:, g - 1:g] if g else -LEAST
                v.tensor_scalar(nmax[:, g:g + 1], gmax[:], -1.0, before, ALU.mult, ALU.min).then_inc(sc_ready, 1)

            def softmax_sum(g):
                dve.wait_ge(p_ready, 1).then_inc(p_ready, -1)
                if g == 0:
                    done(v.tensor_copy(rsum[:, 0:1], gsum[:, 0:1]))
                else:
                    done(v.scalar_tensor_tensor(out=rsum[:, g:g + 1], in0=rsum[:, g - 1:g], scalar=corr[:, g:g + 1],
                                                in1=gsum[:, g:g + 1], op0=ALU.mult, op1=ALU.add))
                if g == NG - 1:
                    done(v.reciprocal(rinv[:], rsum[:, g:g + 1]))

            def tail_history(par):
                dve.wait_ge(acc_ready, 1).then_inc(acc_ready, -1)
                done(v.tensor_scalar(S[:, par, 4, :], acc[:, par, :], rinv[:], None, ALU.mult))
                done(v.tensor_reduce(z5[:], S[:, par, :, :], AX.X, ALU.add))

            def tail_gate_logits():
                w1v = row("se_w1").rearrange("p (j f) -> p j f", j=2)
                done(v.scalar_tensor_tensor(out=se10[:].rearrange("p (j f) -> p j f", j=2),
                                            in0=z5[:].rearrange("p (o f) -> p o f", o=1).to_broadcast([P, 2, FIELDS]),
                                            scalar=1.0 / EMB, in1=w1v, op0=ALU.mult, op1=ALU.mult))
                done(v.tensor_reduce(se2[:], se10[:].rearrange("p (j f) -> p j f", j=2), AX.X, ALU.add))
                done(v.tensor_tensor(se2[:], se2[:], row("se_b1"), ALU.add))
                done(v.tensor_scalar(se2[:], se2[:], 0.0, None, ALU.max))
                w2v = row("se_w2").rearrange("p (f j) -> p f j", j=2)
                done(v.tensor_tensor(se10[:].rearrange("p (f j) -> p f j", j=2),
                                     se2[:].rearrange("p (o j) -> p o j", o=1).to_broadcast([P, FIELDS, 2]), w2v, ALU.mult))
                done(v.tensor_reduce(g5[:], se10[:].rearrange("p (f j) -> p f j", j=2), AX.X, ALU.add))
                done(v.tensor_tensor(g5[:], g5[:], row("se_b2"), ALU.add))
                dve.sem_inc(gate_ready, 1)

            def tail_gate_apply(par):
                dve.wait_ge(gexp_ready, 1).then_inc(gexp_ready, -1)
                done(v.tensor_scalar(g5[:], g5[:], 1.0, None, ALU.add))
                done(v.reciprocal(g5[:], g5[:]))
                done(v.tensor_tensor(S[:, par, :, :], S[:, par, :, :],
                                     g5[:].rearrange("p (f o) -> p f o", o=1).to_broadcast([P, FIELDS, EMB]), ALU.mult))
                dve.sem_inc(se_ready, 1)

            def tail_pairs():
                dve.wait_ge(m_ready, 1).then_inc(m_ready, -1)
                at = FIELDS
                for i in range(4):
                    n = FIELDS - 1 - i
                    v.tensor_tensor(dn[:, at:at + n, :], dn[:, i + 1:FIELDS, :],
                                    mps[:, i * P:(i + 1) * P].rearrange("p (o b) -> p o b", o=1).to_broadcast([P, n, P]),
                                    ALU.mult).then_inc(dve_done, 1)
                    at += n
                dve.wait_ge(dve_done, 4).then_inc(dve_done, -4)
                dve.sem_inc(bank4_free, 1)
                dve.sem_inc(dn_full, 1)

            def w_lo(raw_slot, slot, n=KG * P):
                dve.wait_ge(hi_done, 1).then_inc(hi_done, -1)
                v.tensor_tensor(Wl[:, slot, 0:n], raw[:, raw_slot, 0:n], Wh[:, slot, 0:n].bitcast(F32),
                                ALU.subtract).then_inc(lo_done, 1)

            def w_out():
                dve.wait_ge(lo_done, 1).then_inc(lo_done, -1)
                dve.sem_inc(w_ready, 1)
                dve.sem_inc(raw_free, 1)

            def r_lo(raw_slot, k):
                dve.wait_ge(hi_done, 1).then_inc(hi_done, -1)
                done(v.tensor_tensor(X0l[:, k, :], raw[:, raw_slot, 0:NB], X0h[:, k, :].bitcast(F32), ALU.subtract))
                dve.sem_inc(x_ready, 1)
                dve.sem_inc(raw_free, 1)

            def x_new(layer, n, meanwhile=None):
                v.tensor_tensor(xnew[:], X0h[:, n, :].bitcast(F32), X0l[:, n, :].bitcast(F32), ALU.add).then_inc(dve_done, 1)
                if layer == 1:
                    v.tensor_tensor(xsum[:], X1h[:, n, :].bitcast(F32), X1l[:, n, :].bitcast(F32), ALU.add).then_inc(dve_done, 1)
                if meanwhile:
                    meanwhile()
                dve.wait_ge(dve_done, 1 + layer).then_inc(dve_done, -1 - layer)
                dve.wait_ge(mm_done, 1).then_inc(mm_done, -1)
                a, _ = COLS["cb"]
                bias = cols[:, bass.ds(n + (a + layer * FEATS), 1)]
                done(v.scalar_tensor_tensor(out=xnew[:], in0=xps[:, n % BANKS, :], scalar=bias, in1=xnew[:],
                                            op0=ALU.add, op1=ALU.mult))
                dve.sem_inc(bank_free, 1)
                if layer == 1:
                    done(v.tensor_tensor(xnew[:], xnew[:], xsum[:], ALU.add))
                dve.sem_inc(xnew_ready, 1)

            def x_lo(layer, n):
                Xh, Xl = (X1h, X1l) if layer == 0 else (X0h, X0l)
                dve.wait_ge(xhi_done, 1).then_inc(xhi_done, -1)
                done(v.tensor_tensor(Xl[:, n, :], xnew[:], Xh[:, n, :].bitcast(F32), ALU.subtract))
                dve.sem_inc(x_ready, 1)

            def unit(q, last_layer):
                w_lo(w_slot(q), (q + 2) % RING, H1 if last_layer and q > 0 else KG * P)

            def fc_stats(j, x):
                done(v.bn_stats(fstats[:], x))
                done(v.bn_aggr(fmv[:, j, :], fstats[:]))

            def fc_rstd():
                dve.wait_ge(fsd_ready, 1).then_inc(fsd_ready, -1)
                done(v.reciprocal(frstd[:], fsd[:]))

            def fc_norm(j, x):
                return v.tensor_scalar(x, x, fmv[:, j, 0:1], frstd[:, j:j + 1], ALU.subtract, ALU.mult)

            def fc_bias2(j):
                dve.wait_ge(fmm_ready, 1).then_inc(fmm_ready, -1)
                done(v.tensor_tensor(h2(j), xps[:, FCB, 0:H2], row("b2"), ALU.add))
                dve.sem_inc(bank4_free, 1)

            def fc_logits(c):
                dve.wait_ge(fmm_ready, 1).then_inc(fmm_ready, -1)
                done(v.tensor_scalar(logits[:, bass.ds(c * TPC, TPC)], mps[:, 0:TPC], row("b3"), None, ALU.add))
                dve.sem_inc(bank4_free, 1)

            def step(c, p, dense, more, fc=True):
                fc = fc and p.fc
                grp, tail, head = (p.grp, p.tail, p.head) if more else (None, None, None)
                prev = (p.layer, p.n - 1) if p.n else (0, FEATS - 1) if p.layer else None
                last = p.layer == 1 and p.n == FEATS - 1
                if more and p.open is not None:
                    softmax_max(p.open[0] % 2, p.open[1])
                if dense:
                    if p.layer == 0 and p.n == 0:
                        r_lo(R14_SLOT, FEATS - 1)
                    unit(0, False)
                if dense:
                    if prev is not None:
                        x_new(*prev, w_out)
                    else:
                        w_out()
                if fc and p.n == 0:
                    for j in range(TPC):
                        fc_stats(j, h1[:, j, :])
                    dve.sem_inc(fvar_ready, 1)
                if p.head_before is not None and more:
                    head_T(p.head_before % 2)
                if fc and 1 <= p.n <= TPC:
                    fc_bias2(p.n - 1)
                if fc and 1 <= p.n < TPC:
                    fc_norm(p.n, h1[:, p.n, :]).then_inc(h1n_ready, 1)
                if fc and 1 <= p.n <= TPC:
                    fc_stats(p.n - 1, h2(p.n - 1))
                if fc and p.n == TPC:
                    dve.sem_inc(fvar_ready, 1)
                if tail is not None and p.i == 2:
                    tail_gate_logits()
                if head is not None and p.i == 4:
                    head_target((c + 1) * (TPC // 2) + head // 2, head % 2)
                if grp is not None:
                    add_target(grp % 2)
                    times_target(grp % 2)
                if dense:
                    unit(1, last)
                    w_out()
                if dense and p.layer and p.n == 0:
                    x_lo(*prev)
                if fc and p.n == 0:
                    fc_rstd()
                    fc_norm(0, h1[:, 0, :]).then_inc(h1n_ready, 1)
                if head is not None and p.i == 2:
                    head_var()
                if tail is not None and p.i == 1:
                    tail_history(tail % 2)
                if tail is not None and p.i == 2:
                    tail_gate_apply(tail % 2)
                if grp is not None:
                    add_target(grp % 2)
                if head is not None and p.i == 4:
                    head_tT(head % 2)
                if more and p.follows is not None:
                    times_target(p.follows[0] % 2)
                if dense:
                    unit(2, last)
                    w_out()
                if dense and p.n:
                    x_lo(*prev)
                if fc and p.n == TPC:
                    fc_rstd()
                    for j in range(0, TPC, 2):
                        done(fc_norm(j, h2(j)))
                        fc_norm(j + 1, h2(j + 1)).then_inc(h2n_ready, 1)
                if fc and p.n == 5:
                    fc_logits(c)
                if more and p.open is not None:
                    softmax_sum(p.open[1])
                if tail is not None and p.i == 3:
                    tail_pairs()
                if head is not None and p.i == 2:
                    head_norm()
                if head is not None and p.i == 3:
                    head_mask(head % 2, (c + 1) * TPC + head)

            def plain_step(layer, n, pending, last=False):
                m = n - 1 if pending == layer else FEATS - 1
                unit(0, False)
                w_out()
                x_new(pending, m)
                unit(1, last)
                w_out()
                x_lo(pending, m)
                unit(2, last)
                w_out()

            def w1_stage(more):
                for k in range(FEATS):
                    ws, rs = w1_slots(k, more)
                    if k == 0:
                        x_new(1, FEATS - 1)
                    if k + 2 < FEATS:
                        w_lo(ws, (k + 2) % RING, H1)
                    elif more:
                        w_lo(ws, (k + 2) % RING)
                    if k + 2 < FEATS or more:
                        w_out()
                    if k == 0:
                        x_lo(1, FEATS - 1)
                    if more and k:
                        r_lo(rs, k - 1)
                dve.wait_ge(mm_done, 1).then_inc(mm_done, -1)
                for b in range(TPC):
                    done(v.tensor_tensor(h1[:, b, :], xps[:, b, :], row("b1"), ALU.add))
                    dve.sem_inc(bank_free if b < BANKS else bank4_free, 1)

            def chunk(c, more):
                if more:
                    for p in plan:
                        step(c, p, True, True)
                else:
                    for p in plan[:FC_STEPS]:
                        step(c, p, True, False)
                    with dve.Fori(FC_STEPS, FEATS) as n:
                        plain_step(0, n, 0)
                    plain_step(1, 0, 0)
                    with dve.Fori(1, FEATS - 1) as n:
                        plain_step(1, n, 1)
                    plain_step(1, FEATS - 1, 1, True)
                w1_stage(more)

            dve.sem_inc(raw_free, RING)
            dve.sem_inc(bank_free, BANKS)
            dve.sem_inc(scores_read, 1)
            dve.sem_inc(bank4_free, 1)
            done(v.memset(eps[:], EPS))
            dve.wait_ge(consts_in, NCONST * DMA)
            done(v.tensor_tensor(A02[:], aw1[:, 0, :], aw1[:, 2, :], ALU.add))
            done(v.tensor_copy(A3[:], aw1[:, 3, :]))
            done(v.tensor_tensor(A12[:], aw1[:, 1, :], aw1[:, 2, :], ALU.subtract))
            done(v.tensor_scalar(col("cb", 0, FEATS), col("cb", 0, FEATS), 1.0, None, ALU.add))
            dve.sem_inc(consts_ok, 2)
            for u in range(2):
                w_lo(u, u)
                w_out()
            dve.wait_ge(idx_in, DMA)
            for p in plan:
                step(-1, p, False, True, False)
            for k in range(FEATS - 1):
                r_lo((2 + k) % RING, k)
            done(v.memset(h1, 0.0))
            with dve.Fori(0, nchunks - 1) as c:
                chunk(c, True)
            chunk(nchunks - 1, False)
            for p in plan[:FC_STEPS]:
                step(nchunks, p, False, False)
            dve.sem_inc(logits_ready, 1)
            dve.wait_ge(lexp_ready, 1).then_inc(lexp_ready, -1)
            done(v.tensor_scalar(probs[:], probs[:], 1.0, None, ALU.add))
            done(v.reciprocal(probs[:], probs[:]))
            dve.sem_inc(probs_ready, 1)
            dve.wait_ge(probsT_ready, 1).then_inc(probsT_ready, -1)
            done(v.tensor_copy(xi[0:ntiles, :], xps[0:ntiles, FCB, 0:P]))
            dve.sem_inc(res_ready, 1)


def kernel(**inputs):
    import numpy as np
    import concourse.bacc as bacc
    from concourse.bass_utils import run_bass_kernel_spmd as run

    x = {k.removeprefix("L0_rec_"): np.asarray(a) for k, a in inputs.items()}
    batch = x["r_item_seq"].shape[0]
    tiles = batch // P

    def column(name):
        return x[name].reshape(-1, 1)

    idx = np.concatenate([x["r_item_seq"], column("r_item_id"), column("r_likes_level"), column("r_views_level")], axis=1)
    rows = {"mm_b": x["mm_b"], "mm_g": x["mm_ln_g"], "mm_lb": x["mm_ln_b"], "b1": x["b1"],
            "b2": x["b2"], "se_w1": x["se_w1"].T, "se_b1": x["se_b1"], "se_w2": x["se_w2"].T, "se_b2": x["se_b2"],
            "ab2": x["ab2"], "b3": x["b3"]}
    cols = {"g1": x["ln1g"], "lb1": x["ln1b"], "g2": x["ln2g"], "lb2": x["ln2b"], "w3": x["w3"], "cb": x["cross_bias"],
            "ab1": np.concatenate([x["ab1"].reshape(-1), x["aw2"].reshape(-1)]),
            "aw2": np.concatenate([x["aw2"].reshape(-1), x["ab1"].reshape(-1)])}
    host = {
        "idx": idx.reshape(tiles, P, SEQ + 3).transpose(1, 0, 2),
        "item_table": x["item_table"],
        "cate_table": x["cate_table"],
        "embT": x["r_item_emb_d128"].T,
        "rows": np.broadcast_to(np.concatenate([rows[k].reshape(-1) for k in ROWS]), (P, NROWS)),
        "cols": np.concatenate([cols[k].reshape(-1, P).T for k in COLS], axis=1),
        "mm_w": x["mm_w"],
        "aw1": x["aw1"],
        "bil_W": x["bil_W"],
        "cross_K": x["cross_K"].reshape(2, UNITS, KG, P, FEATS, P).transpose(0, 4, 1, 3, 2, 5)
                   .reshape(2 * FEATS * UNITS, P, KG * P),
        "w1": x["w1"],
        "w2": x["w2"],
    }
    nc = bacc.Bacc("TRN2", target_bir_lowering=False, num_devices=1, dynamic_dma_scratch_size=8192)
    arrays, args = {}, []
    for name, a in host.items():
        a = np.ascontiguousarray(a)
        arrays[f"in_{name}"] = a
        args.append(nc.dram_tensor(f"in_{name}", a.shape, mybir.dt.from_np(a.dtype), kind="ExternalInput").ap())
    out = nc.dram_tensor("out_probs", (tiles, P), F32, kind="ExternalOutput").ap()
    build(nc, *args, out, tiles)
    r = run(nc, [arrays], core_ids=[0])
    return r.results[0]["out_probs"].reshape(batch)
```

```python
from contextlib import ExitStack

import concourse.bass as bass
from concourse import mybir

ALU = mybir.AluOpType
ACT = mybir.ActivationFunctionType
AX = mybir.AxisListType
F32 = mybir.dt.float32
F32R = mybir.dt.float32r
I32 = mybir.dt.int32

P = 128
EMB = 128
SEQ = 50
HID = 64
FIELDS = 5
FEATS = FIELDS + FIELDS * (FIELDS - 1) // 2
TPC = 4
NB = TPC * P
GRP = 10
SUB = 5
NG = SEQ // GRP
KG = 5
UNITS = FEATS // KG
H1 = 512
H2 = 256
RING = 3
BANKS = 3
EPS = 1e-5
LEAST = -3.0e38
MASKED = -1.0e9
DMA = 16

ROWS = {}
_at = 0
for _name, _n in (("mm_b", EMB), ("mm_g", EMB), ("mm_lb", EMB), ("ab1", HID), ("aw2", HID), ("b1", H1),
                  ("b2", H2), ("se_w1", 2 * FIELDS), ("se_b1", 2), ("se_w2", 2 * FIELDS), ("se_b2", FIELDS),
                  ("ab2", 1), ("b3", 1)):
    ROWS[_name] = (_at, _at + _n)
    _at += _n
NROWS = _at
COLS = {}
_at = 0
for _name, _n in (("g1", 4), ("lb1", 4), ("g2", 2), ("lb2", 2), ("w3", 2), ("cb", 2 * FEATS)):
    COLS[_name] = (_at, _at + _n)
    _at += _n
NCOLS = _at

FC_STEPS = 6
SEGMENTS = [(0, 0, None, None, 0), (0, 1, 0, None, 1), (0, 2, 1, 0, 2), (1, 0, 2, 1, 3), (1, 1, 3, 2, None),
            (1, 2, None, 3, None)]


class Step:

    def __init__(self, layer, n, grp, g, follows, opened, tail, head, head_before, fc):
        self.layer, self.n, self.grp, self.g, self.follows, self.open = layer, n, grp, g, follows, opened
        self.tail, self.head, self.fc = tail, head, fc
        self.i = n % 5
        self.head_before = head_before


def steps():
    plan = []
    for at, (layer, fifth, grp, tail, head) in enumerate(SEGMENTS):
        for i in range(5):
            after = SEGMENTS[at + (i == 4)][2] if at + (i == 4) < len(SEGMENTS) else None
            before = SEGMENTS[at - (i == 0)][2] if at - (i == 0) >= 0 else None
            plan.append(Step(layer, 5 * fifth + i, grp, i, None if after is None else (after, (i + 1) % 5),
                             None if before is None else (before, (i - 1) % 5), tail, head,
                             SEGMENTS[at - 1][4] if at and i == 0 else None, layer == 0 and 5 * fifth + i < FC_STEPS))
    return plan


def link(eng, sem, ins):
    ins.then_inc(sem, 1)
    eng.wait_ge(sem, 1).then_inc(sem, -1)


def build(nc, idx_d, table_d, cate_d, embT_d, rows_d, cols_d, mmw_d, aw1_d, bil_d, kx_d, w1_d, w2_d, out_d, ntiles):
    nchunks = ntiles // TPC
    with ExitStack() as ctx:
        def sb(name, shape, dt=F32):
            return ctx.enter_context(nc.sbuf_tensor(name, shape, dt))

        def ps(name, shape):
            return ctx.enter_context(nc.psum_tensor(name, shape, F32))

        def sem(name):
            return ctx.enter_context(nc.semaphore(name))

        dnn_d = nc.dram_tensor("dnn_scratch", (nchunks, FEATS, P, TPC, P), F32, kind="Internal").ap()

        xps = ps("xps", [P, BANKS + 1, 512])
        FCB = BANKS
        mps = xps[:, FCB, :]
        aps = ps("aps", [P, 2 * 512])
        tps = aps[:, 0:SUB * P]
        hps = ps("hps", [P, 2, 512])

        X0h = sb("X0h", [P, FEATS, NB], F32R)
        X0l = sb("X0l", [P, FEATS, NB], F32R)
        X1h = sb("X1h", [P, FEATS, NB], F32R)
        X1l = sb("X1l", [P, FEATS, NB], F32R)
        raw = sb("raw", [P, RING, KG * P])
        Wh = sb("Wh", [P, RING, KG * P], F32R)
        Wl = sb("Wl", [P, RING, KG * P], F32R)
        xnew = sb("xnew", [P, NB])
        e = sb("e", [P, NG * GRP, EMB])
        eT = sb("eT", [P, SUB * P])
        teT = sb("teT", [P, SUB * P])
        eTs = (eT[:], raw[:, 2, 0:SUB * P])
        teTs = (teT[:], raw[:, 0, 0:SUB * P])
        xsum = sb("xsum", [P, NB])
        idx_all = sb("idx_all", [P, ntiles, SEQ + 3], I32)
        idx_cur = sb("idx_cur", [P, 2, SEQ + 3], I32)
        S = sb("S", [P, 2, FIELDS, EMB])
        tT = sb("tT", [P, 2, P])
        Tt = sb("Tt", [P, 2, HID])
        keep = sb("keep", [P, 2, SEQ])
        mbias = sb("mbias", [P, 2, SEQ])
        hid = sb("hid", [P, SUB, HID])
        sc = sb("sc", [P, NG, GRP])
        pw = sb("pw", [P, GRP])
        gmax = sb("gmax", [P, 1])
        nmax = sb("nmax", [P, NG])
        corr = sb("corr", [P, NG])
        gsum = sb("gsum", [P, NG])
        rsum = sb("rsum", [P, NG])
        sd = sb("sd", [P, 1])
        rinv = sb("rinv", [P, 1])
        acc = sb("acc", [P, 2, EMB])
        emb = sb("emb", [P, P])
        xi = sb("xi", [P, EMB])
        tgt = sb("tgt", [P, EMB])
        stats = sb("stats", [P, 6])
        mv = sb("mv", [P, 2])
        rstd = sb("rstd", [P, 1])
        fstats = sb("fstats", [P, 6])
        fmv = sb("fmv", [P, TPC, 2])
        fsd = sb("fsd", [P, TPC])
        frstd = sb("frstd", [P, TPC])
        z5 = sb("z5", [P, FIELDS])
        se10 = sb("se10", [P, 2 * FIELDS])
        se2 = sb("se2", [P, 2])
        g5 = sb("g5", [P, FIELDS])
        dn = sb("dn", [P, TPC * H1 // P, P])
        h1 = dn[:].rearrange("p f b -> p (f b)").rearrange("p (t n) -> p t n", t=TPC)

        def h1_T(j):
            return h1[:, j, :].rearrange("p (k b) -> p k b", b=P)

        def h2(j):
            return h1[:, j, 0:H2]

        def g2T(pair, k):
            return h1[:, 2 * pair:2 * pair + 2, H2 + k * P:H2 + (k + 1) * P]

        logits = sb("logits", [P, TPC * (nchunks + 1)])
        probs = sb("probs", [P, ntiles])
        ident = sb("ident", [P, P])
        eps = sb("eps", [P, 1])
        rows = sb("rows", [P, NROWS])
        cols = sb("cols", [P, NCOLS])
        mmw = sb("mmw", [P, EMB])
        A3 = sb("A3", [P, HID])
        A02 = sb("A02", [P, HID])
        A12 = sb("A12", [P, HID])
        bil = sb("bil", [P, 4, EMB])
        w2 = sb("w2", [P, H1 // P, H2])

        aw1 = xsum[:, 0:4 * HID].rearrange("p (q n) -> p q n", q=4)

        def row(name):
            a, b = ROWS[name]
            return rows[:, a:b]

        def col(name, k, n=1):
            a, _ = COLS[name]
            return cols[:, a + k:a + k + n]

        consts_in = sem("consts_in")
        late_in = sem("late_in")
        consts_ok = sem("consts_ok")
        ident_ok = sem("ident_ok")
        ident_z = sem("ident_z")
        idx_in = sem("idx_in")
        act_done = sem("act_done")
        dve_done = sem("dve_done")
        pool_done = sem("pool_done")
        raw_landed = [sem(f"raw_landed{i}") for i in range(RING)]
        raw_free = sem("raw_free")
        split_free = sem("split_free")
        hi_done = sem("hi_done")
        w_ready = sem("w_ready")
        x_ready = sem("x_ready")
        x0_free = sem("x0_free")
        bank_free = sem("bank_free")
        mm_done = sem("mm_done")
        xnew_ready = sem("xnew_ready")
        xhi_done = sem("xhi_done")
        emb_landed = sem("emb_landed")
        dnn_stored = sem("dnn_stored")
        dnn_ready = sem("dnn_ready")
        feat_landed = [sem(f"feat_landed{i}") for i in range(2)]
        e_landed = [sem(f"e_landed{i}") for i in range(NG)]
        S_free = sem("S_free")
        tp_ready = sem("tp_ready")
        tp_free = sem("tp_free")
        eT_ready = sem("eT_ready")
        eT_free = sem("eT_free")
        te_ready = sem("te_ready")
        h_ready = sem("h_ready")
        sc_ready = sem("sc_ready")
        p_ready = sem("p_ready")
        weighed = sem("weighed")
        e_free = sem("e_free")
        acc_scaled = sem("acc_scaled")
        acc_ready = sem("acc_ready")
        sum_done = sem("sum_done")
        scaled = sem("scaled")
        hid_done = sem("hid_done")
        hist_done = sem("hist_done")
        lo_done = sem("lo_done")
        bank4_free = sem("bank4_free")
        m_ready = sem("m_ready")
        xi_ready = sem("xi_ready")
        var_ready = sem("var_ready")
        sd_ready = sem("sd_ready")
        fvar_ready = sem("fvar_ready")
        fsd_ready = sem("fsd_ready")
        img_ready = sem("img_ready")
        tgt_ready = sem("tgt_ready")
        tT_ready = sem("tT_ready")
        gate_ready = sem("gate_ready")
        gexp_ready = sem("gexp_ready")
        se_ready = sem("se_ready")
        seT_ready = sem("seT_ready")
        dn_full = sem("dn_full")
        h1n_ready = sem("h1n_ready")
        fT_ready = sem("fT_ready")
        g_ready = sem("g_ready")
        fmm_ready = sem("fmm_ready")
        h2n_ready = sem("h2n_ready")
        logits_ready = sem("logits_ready")
        lexp_ready = sem("lexp_ready")
        probs_ready = sem("probs_ready")
        probsT_ready = sem("probsT_ready")
        res_ready = sem("res_ready")
        out_stored = sem("out_stored")

        NCONST = 4
        plan = steps()

        UL = FEATS * UNITS
        DIRECT = FEATS - 3
        START = 2 + FEATS - 1 - DIRECT
        assert START % RING == 1 and (1 + 2 * UL + 2 * FEATS - 1) % RING == 0
        R14_SLOT = START % RING

        def w_slot(q):
            return (q + 2) % RING

        def w1_slots(k, refill):
            at = START + 2 * UL + 1 + (2 * k - 1 if refill and k else k)
            return at % RING, (at + 1) % RING

        def e_sub(g, u, s):
            return e[:, g * GRP + u * SUB + s, :]

        block = ctx.enter_context(nc.Block())

        @block.sync
        def _(sp):
            def load(slot, src, n):
                sp.wait_ge(raw_free, 1).then_inc(raw_free, -1)
                sp.dma_start(raw[:, slot, 0:n], src).then_inc(raw_landed[slot], DMA)

            def k_unit(u, slot):
                load(slot, kx_d[u], KG * P)

            def w1_unit(k, slot):
                load(slot, w1_d[k * P:(k + 1) * P, :], H1)

            def r_unit(c, k, slot):
                load(slot, dnn_d[c, k].rearrange("p t b -> p (t b)"), NB)

            sp.dma_start(idx_all[:], idx_d).then_inc(idx_in, DMA)
            sp.dma_start(mmw[:], mmw_d).then_inc(consts_in, DMA)
            sp.dma_start(rows[:], rows_d).then_inc(consts_in, DMA)
            sp.dma_start(cols[:], cols_d).then_inc(consts_in, DMA)
            sp.dma_start(aw1, aw1_d.rearrange("(q p) n -> p q n", p=P)).then_inc(consts_in, DMA)
            sp.dma_start(bil[:], bil_d.rearrange("i d e -> d i e")).then_inc(late_in, DMA)
            sp.dma_start(w2[:], w2_d.rearrange("(k p) n -> p k n", p=P)).then_inc(late_in, DMA)
            k_unit(0, 0)
            k_unit(1, 1)
            sp.wait_ge(dnn_ready, TPC).then_inc(dnn_ready, -TPC)
            for k in range(DIRECT, FEATS - 1):
                r_unit(0, k, (2 + k - DIRECT) % RING)

            def chunk(c, more):
                r_unit(c, FEATS - 1, R14_SLOT)
                with sp.Fori(0, (2 * UL - 3) // RING) as i:
                    for j in range(RING):
                        k_unit(i * RING + 2 + j, (2 + j) % RING)
                k_unit(2 * UL - 1, (2 * UL - 1) % RING)
                w1_unit(0, w_slot(2 * UL - 2))
                w1_unit(1, w_slot(2 * UL - 1))
                for k in range(FEATS):
                    ws, rs = w1_slots(k, more)
                    if k + 2 < FEATS:
                        w1_unit(k + 2, ws)
                    elif more:
                        k_unit(k + 2 - FEATS, ws)
                    if more and k:
                        if k == 1:
                            sp.wait_ge(dnn_ready, TPC).then_inc(dnn_ready, -TPC)
                        r_unit(c + 1, k - 1, rs)

            with sp.Fori(0, nchunks - 1) as c:
                chunk(c, True)
            chunk(nchunks - 1, False)
            sp.wait_ge(res_ready, 1).then_inc(res_ready, -1)
            sp.dma_start(out_d, xi[0:ntiles, :]).then_inc(out_stored, DMA)
            sp.wait_ge(out_stored, DMA)
        @block.gpsimd
        def _(pool):
            nc.gpsimd.memset(ident[:], 0.0).then_inc(ident_z, 1)
            pool.wait_ge(ident_z, 1).then_inc(ident_z, -1)
            nc.gpsimd.affine_select(out=ident[:], in_=ident[:], compare_op=ALU.not_equal, fill=1.0, base=0,
                                    pattern=[[-1, P]], channel_multiplier=1).then_inc(ident_ok, 1)
            pool.wait_ge(idx_in, DMA)

            def gather(dst, table, par, s, landed):
                nc.gpsimd.indirect_dma_start(
                    out=dst, out_offset=None, in_=table,
                    in_offset=bass.IndirectOffsetOnAxis(ap=idx_cur[:, par, s:s + 1], axis=0),
                ).then_inc(landed, DMA)

            def indices(t, par):
                link(pool, pool_done, nc.gpsimd.tensor_copy(idx_cur[:, par, :], idx_all[:, t, :]))

            def features(par):
                pool.wait_ge(S_free, 1).then_inc(S_free, -1)
                gather(S[:, par, 2, :], table_d, par, SEQ, feat_landed[par])
                gather(S[:, par, 0, :], cate_d, par, SEQ + 1, feat_landed[par])
                gather(S[:, par, 1, :], cate_d, par, SEQ + 2, feat_landed[par])

            def embeddings(par, g):
                for s in range(GRP):
                    gather(e[:, g * GRP + s, :], table_d, par, g * GRP + s, e_landed[g])

            def history(par, g):
                a = g * GRP
                own = acc[:, par, :] if g == 0 else e[:, a, :]
                pool.wait_ge(weighed, 1).then_inc(weighed, -1)
                if g:
                    nc.gpsimd.tensor_scalar(acc[:, par, :], acc[:, par, :], corr[:, g:g + 1], None,
                                            ALU.mult).then_inc(acc_scaled, 1)
                for n in (5, 2):
                    x, y = e[:, a:a + n, :], e[:, a + n:a + 2 * n, :]
                    link(pool, pool_done, nc.gpsimd.tensor_tensor(x, x, y, ALU.add))
                link(pool, pool_done, nc.gpsimd.tensor_tensor(e[:, a, :], e[:, a, :], e[:, a + 1, :], ALU.add))
                link(pool, pool_done, nc.gpsimd.tensor_tensor(own, e[:, a, :], e[:, a + 4, :], ALU.add))
                if g:
                    pool.wait_ge(acc_scaled, 1).then_inc(acc_scaled, -1)
                    link(pool, pool_done, nc.gpsimd.tensor_tensor(acc[:, par, :], acc[:, par, :], e[:, a, :], ALU.add))
                if g == NG - 1:
                    pool.sem_inc(acc_ready, 1)

            def tile(t, par, more, sums=True, features_at=2):
                if more and features_at is not None:
                    indices(t + 1, 1 - par)
                for g in range(NG):
                    if sums:
                        history(par, g)
                    else:
                        pool.wait_ge(e_free, 1).then_inc(e_free, -1)
                    if more:
                        if g == features_at:
                            features(1 - par)
                        embeddings(1 - par, g)

            indices(0, 0)
            features(0)
            for g in range(NG):
                embeddings(0, g)
            indices(1, 1)
            features(1)
            tile(0, 0, True, False, None)
            for t in range(1, TPC):
                tile(t, t % 2, True, False, 1)
            with pool.Fori(TPC // 2, ntiles // 2 - 1) as i:
                for par in range(2):
                    tile(i * 2 + par, par, True)
            tile(ntiles - 2, 0, True)
            tile(ntiles - 1, 1, False)

        @block.tensor
        def _(pe):
            mm = nc.tensor.matmul

            def transposes(t, g, u):
                if u == 0:
                    pe.wait_ge(e_landed[g], (t + 1) * (DMA * GRP))
                pe.wait_ge(tp_free, 1).then_inc(tp_free, -1)
                for s in range(SUB):
                    last = nc.tensor.transpose(tps[:, s * P:(s + 1) * P], e_sub(g, u, s), ident[:])
                last.then_inc(tp_ready, 1)

            def hidden(u, at=0):
                pe.wait_ge(te_ready, 1).then_inc(te_ready, -1)
                for s in range(SUB):
                    o = hps[:, u, s * HID:(s + 1) * HID]
                    mm(o, eTs[at][:, s * P:(s + 1) * P], A12[:], start=True, stop=False)
                    last = mm(o, teTs[at][:, s * P:(s + 1) * P], A3[:], start=False, stop=True)
                last.then_inc(h_ready, 1)

            def head_mm():
                pe.wait_ge(emb_landed, DMA).then_inc(emb_landed, -DMA)
                pe.wait_ge(bank4_free, 1).then_inc(bank4_free, -1)
                mm(mps[:, 0:P], emb[:], mmw[:], start=True, stop=True).then_inc(m_ready, 1)

            def head_turn():
                pe.wait_ge(tgt_ready, 1).then_inc(tgt_ready, -1)
                pe.wait_ge(bank4_free, 1).then_inc(bank4_free, -1)
                nc.tensor.transpose(mps[:, 0:P], tgt[:], ident[:]).then_inc(m_ready, 1)

            def head_share(par):
                pe.wait_ge(tT_ready, 1).then_inc(tT_ready, -1)
                mm(mps[:, P:P + HID], tT[:, par, :], A02[:], start=True, stop=True).then_inc(m_ready, 1)

            def tail_turn(par):
                pe.wait_ge(se_ready, 1).then_inc(se_ready, -1)
                pe.wait_ge(tp_free, 1).then_inc(tp_free, -1)
                for f in range(FIELDS):
                    last = nc.tensor.transpose(tps[:, f * P:(f + 1) * P], S[:, par, f, :], ident[:])
                last.then_inc(tp_ready, 1)

            def tail_bilinear():
                pe.wait_ge(seT_ready, 1).then_inc(seT_ready, -1)
                pe.wait_ge(bank4_free, 1).then_inc(bank4_free, -1)
                for i in range(4):
                    last = mm(mps[:, i * P:(i + 1) * P], bil[:, i, :], dn[:, i, :], start=True, stop=True)
                last.then_inc(m_ready, 1)

            def products(layer, n, kg, first):
                Xh, Xl = (X0h, X0l) if layer == 0 else (X1h, X1l)
                out = xps[:, n % BANKS, :]
                if kg == 0:
                    pe.wait_ge(bank_free, 1).then_inc(bank_free, -1)
                pe.wait_ge(w_ready, 1).then_inc(w_ready, -1)
                for i in range(KG):
                    k = kg * KG + i
                    if first:
                        pe.wait_ge(x_ready, 1).then_inc(x_ready, -1)
                    wh, wl = Wh[:, kg, i * P:(i + 1) * P], Wl[:, kg, i * P:(i + 1) * P]
                    m0 = mm(out, wh, Xh[:, k, :], start=(k == 0), stop=False)
                    m1 = mm(out, wh, Xl[:, k, :], start=False, stop=False)
                    m2 = mm(out, wl, Xh[:, k, :], start=False, stop=(k == FEATS - 1))
                    if i == 0:
                        m0.then_inc(split_free, 1)
                        if layer == 0 and first and kg == 0:
                            m1.then_inc(x0_free, 1)
                if kg == UNITS - 1:
                    m2.then_inc(mm_done, 1)

            def w1_products(more):
                for k in range(FEATS):
                    pe.wait_ge(w_ready, 1).then_inc(w_ready, -1)
                    pe.wait_ge(x_ready, 1).then_inc(x_ready, -1)
                    s = k % RING
                    for b in (0, 1, 3, 2):
                        if k == 0 and b < BANKS:
                            pe.wait_ge(bank_free, 1).then_inc(bank_free, -1)
                        elif k == 0:
                            pe.wait_ge(bank4_free, 1).then_inc(bank4_free, -1)
                        out = xps[:, b, :]
                        xh, xl = X0h[:, k, b * P:(b + 1) * P], X0l[:, k, b * P:(b + 1) * P]
                        m0 = mm(out, xh, Wh[:, s, 0:H1], start=(k == 0), stop=False)
                        m1 = mm(out, xh, Wl[:, s, 0:H1], start=False, stop=False)
                        m2 = mm(out, xl, Wh[:, s, 0:H1], start=False, stop=(k == FEATS - 1))
                        if b == 0:
                            m0.then_inc(split_free, 1)
                            if more and k:
                                m1.then_inc(x0_free, 1)
                            if k == FEATS - 1:
                                m2.then_inc(mm_done, 1)
                m2.then_inc(mm_done, 1)

            def fc_turn1(j, bank=FCB):
                pe.wait_ge(h1n_ready, 1).then_inc(h1n_ready, -1)
                if bank == FCB:
                    pe.wait_ge(bank4_free, 1).then_inc(bank4_free, -1)
                for k in range(H1 // P):
                    last = nc.tensor.transpose(xps[:, bank, k * P:(k + 1) * P], h1[:, j, k * P:(k + 1) * P], ident[:])
                last.then_inc(fT_ready, 1)

            def fc_w2(j, bank=FCB):
                pe.wait_ge(g_ready, 1).then_inc(g_ready, -1)
                if bank == FCB:
                    pe.wait_ge(bank4_free, 1).then_inc(bank4_free, -1)
                for k in range(H1 // P):
                    last = mm(xps[:, bank, 0:H2], h1_T(j)[:, k, :], w2[:, k, :], start=(k == 0), stop=(k == H1 // P - 1))
                last.then_inc(fmm_ready, 1)

            def fc_turn2(pair, bank=FCB):
                pe.wait_ge(h2n_ready, 1).then_inc(h2n_ready, -1)
                if bank == FCB:
                    pe.wait_ge(bank4_free, 1).then_inc(bank4_free, -1)
                for k in range(H2 // P):
                    for i in range(2):
                        at = (2 * k + i) * P
                        last = nc.tensor.transpose(xps[:, bank, at:at + P], h2(2 * pair + i)[:, k * P:(k + 1) * P], ident[:])
                last.then_inc(fT_ready, 1)

            def fc_w3():
                pe.wait_ge(g_ready, 2).then_inc(g_ready, -2)
                pe.wait_ge(bank4_free, 1).then_inc(bank4_free, -1)
                for j in range(TPC):
                    for k in range(H2 // P):
                        last = mm(mps[:, j:j + 1], g2T(j // 2, k)[:, j % 2, :], col("w3", k), start=(k == 0),
                                  stop=(k == H2 // P - 1))
                last.then_inc(fmm_ready, 1)

            def opening_step(p):
                if p.grp is not None:
                    transposes(p.grp, p.g, 1)
                    hidden(0)
                if p.head is not None and p.i == 2:
                    head_mm()
                if p.tail is not None and p.i == 3:
                    tail_bilinear()
                if p.follows is not None:
                    transposes(p.follows[0], p.follows[1], 0)
                if p.head is not None and p.i == 4:
                    head_turn()
                if p.grp is not None:
                    hidden(1, 1)
                if p.tail is not None and p.i == 2:
                    tail_turn(p.tail % 2)
                if p.head is not None and p.i == 4:
                    head_share(p.head % 2)

            def step(c, p, more):
                fc = p.fc
                first = p.n == 0
                grp, tail, head = (p.grp, p.tail, p.head) if more else (None, None, None)
                products(p.layer, p.n, 0, first)
                if grp is not None:
                    transposes((c + 1) * TPC + grp, p.g, 1)
                    hidden(0)
                if fc and p.n == 5:
                    fc_turn2(0)
                if fc and p.n == 1:
                    fc_turn1(0)
                if fc and 1 < p.n <= TPC:
                    fc_w2(p.n - 1)
                products(p.layer, p.n, 1, first)
                if grp is not None:
                    hidden(1)
                if tail is not None and p.i == 3:
                    tail_bilinear()
                if fc and p.n == 1:
                    fc_w2(0)
                if head is not None and p.i == 2:
                    head_mm()
                if fc and p.n == 5:
                    fc_turn2(1)
                if more and p.follows is not None:
                    transposes((c + 1) * TPC + p.follows[0], p.follows[1], 0)
                if head is not None and p.i == 4:
                    head_turn()
                products(p.layer, p.n, 2, first)
                if tail is not None and p.i == 2:
                    tail_turn(tail % 2)
                if head is not None and p.i == 4:
                    head_share(head % 2)
                if fc and 1 <= p.n < TPC:
                    fc_turn1(p.n)
                if fc and p.n == 5:
                    fc_w3()

            def chunk(c, more):
                if more:
                    for p in plan:
                        step(c, p, True)
                else:
                    for p in plan[:FC_STEPS]:
                        step(c, p, False)
                    with pe.Fori(FC_STEPS, FEATS) as n:
                        for kg in range(UNITS):
                            products(0, n, kg, False)
                    for kg in range(UNITS):
                        products(1, 0, kg, True)
                    with pe.Fori(1, FEATS) as n:
                        for kg in range(UNITS):
                            products(1, n, kg, False)
                w1_products(more)

            pe.wait_ge(ident_ok, 1)
            pe.wait_ge(consts_ok, 1)
            for p in plan[:TPC]:
                opening_step(p)
            pe.wait_ge(late_in, 2 * DMA)
            for p in plan[TPC:]:
                opening_step(p)
            with pe.Fori(0, nchunks - 1) as c:
                chunk(c, True)
            chunk(nchunks - 1, False)
            for j in range(TPC + 1):
                if j < TPC:
                    fc_turn1(j, j)
                if j:
                    fc_w2(j - 1, j - 1)
            fc_turn2(0, 0)
            fc_turn2(1, 1)
            fc_w3()
            pe.wait_ge(probs_ready, 1).then_inc(probs_ready, -1)
            pe.wait_ge(bank4_free, 1).then_inc(bank4_free, -1)
            nc.tensor.transpose(xps[0:ntiles, FCB, 0:P], probs[:, :], ident[:]).then_inc(probsT_ready, 1)

        @block.scalar
        def _(act):
            af = nc.scalar.activation

            def done(ins):
                link(act, act_done, ins)

            def copy_eT(at=0):
                act.wait_ge(tp_ready, 1).then_inc(tp_ready, -1)
                act.wait_ge(eT_free, 1).then_inc(eT_free, -1)
                done(af(eTs[at], tps, ACT.Copy))
                act.sem_inc(tp_free, 1)
                act.sem_inc(eT_ready, 1)

            def exps(g):
                act.wait_ge(sc_ready, 1).then_inc(sc_ready, -1)
                if g:
                    af(corr[:, g:g + 1], nmax[:, g - 1:g], ACT.Exp, scale=-1.0, bias=nmax[:, g:g + 1])
                done(af(pw[:], sc[:, g, :], ACT.Exp, bias=nmax[:, g:g + 1], accum_out=gsum[:, g:g + 1]))
                act.sem_inc(p_ready, 1)

            def weigh(g):
                for s in range(GRP):
                    x = e[:, g * GRP + s, :]
                    last = af(x, x, ACT.Copy, scale=pw[:, s:s + 1])
                last.then_inc(weighed, 1)

            def head_load(t):
                act.dma_start(emb[:], embT_d[:, bass.ds(t * P, P)]).then_inc(emb_landed, DMA)

            def head_sd():
                act.wait_ge(var_ready, 1).then_inc(var_ready, -1)
                af(sd[:], mv[:, 1:2], ACT.Sqrt, bias=eps[:]).then_inc(sd_ready, 1)

            def head_gelu(par):
                act.wait_ge(xi_ready, 1).then_inc(xi_ready, -1)
                af(S[:, par, 3, :], xi[:], ACT.Gelu).then_inc(img_ready, 1)

            def tail_gate():
                act.wait_ge(gate_ready, 1).then_inc(gate_ready, -1)
                af(g5[:], g5[:], ACT.Exp, scale=-1.0).then_inc(gexp_ready, 1)

            def tail_copy():
                act.wait_ge(tp_ready, 1).then_inc(tp_ready, -1)
                done(af(dn[:, 0:FIELDS, :].rearrange("p s b -> p (s b)"), tps, ACT.Copy))
                act.sem_inc(tp_free, 1)
                act.sem_inc(S_free, 1)
                act.sem_inc(seT_ready, 1)

            def tail_store(c, j):
                act.wait_ge(dn_full, 1).then_inc(dn_full, -1)
                act.dma_start(dnn_d[c, :, :, j, :].rearrange("f p b -> p f b"), dn[:, 0:FEATS, :]).then_inc(dnn_stored, DMA)

            def tail_hi(j):
                af(X0h[:, 0:DIRECT, j * P:(j + 1) * P], dn[:, 0:DIRECT, :], ACT.Copy).then_inc(hi_done, 1)

            def tail_settle():
                act.wait_ge(dnn_stored, DMA).then_inc(dnn_stored, -DMA)
                act.sem_inc(dnn_ready, 1)

            def w_hi(raw_slot, slot, n=KG * P):
                act.wait_ge(raw_landed[raw_slot], DMA).then_inc(raw_landed[raw_slot], -DMA)
                act.wait_ge(split_free, 1).then_inc(split_free, -1)
                af(Wh[:, slot, 0:n], raw[:, raw_slot, 0:n], ACT.Copy).then_inc(hi_done, 1)

            def r_hi(raw_slot, k, reused=True):
                act.wait_ge(raw_landed[raw_slot], DMA).then_inc(raw_landed[raw_slot], -DMA)
                if reused:
                    act.wait_ge(x0_free, 1).then_inc(x0_free, -1)
                af(X0h[:, k, :], raw[:, raw_slot, 0:NB], ACT.Copy).then_inc(hi_done, 1)

            def x_hi(layer, n):
                act.wait_ge(xnew_ready, 1).then_inc(xnew_ready, -1)
                Xh = X1h if layer == 0 else X0h
                af(Xh[:, n, :], xnew[:], ACT.Copy).then_inc(xhi_done, 1)

            def fc_sd():
                act.wait_ge(fvar_ready, 1).then_inc(fvar_ready, -1)
                af(fsd[:], fmv[:, :, 1], ACT.Sqrt, bias=eps[:]).then_inc(fsd_ready, 1)

            def fc_gelu1(j, bank=FCB):
                act.wait_ge(fT_ready, 1).then_inc(fT_ready, -1)
                for k in range(H1 // P):
                    last = af(h1_T(j)[:, k, :], xps[:, bank, k * P:(k + 1) * P], ACT.Gelu,
                              scale=col("g1", k), bias=col("lb1", k))
                done(last)
                if bank == FCB:
                    act.sem_inc(bank4_free, 1)
                act.sem_inc(g_ready, 1)

            def fc_gelu2(pair, bank=FCB):
                act.wait_ge(fT_ready, 1).then_inc(fT_ready, -1)
                for k in range(H2 // P):
                    last = af(g2T(pair, k), xps[:, bank, 2 * k * P:2 * (k + 1) * P].rearrange("p (t b) -> p t b", t=2),
                              ACT.Gelu, scale=col("g2", k), bias=col("lb2", k))
                done(last)
                if bank == FCB:
                    act.sem_inc(bank4_free, 1)
                act.sem_inc(g_ready, 1)

            def unit(q, last_layer):
                w_hi(w_slot(q), (q + 2) % RING, H1 if last_layer and q > 0 else KG * P)

            def opening_step(p):
                if p.head and p.i == 0:
                    head_load(p.head)
                if p.grp is not None:
                    copy_eT(1)
                if p.open is not None:
                    exps(p.open[1])
                if p.tail is not None and p.i == 2:
                    tail_gate()
                if p.open is not None:
                    weigh(p.open[1])
                if p.tail is not None and p.i == 4:
                    tail_store(0, p.tail)
                if p.follows is not None:
                    copy_eT()
                if p.tail is not None and p.i == 2:
                    tail_copy()
                if p.head is not None and p.i == 3:
                    head_gelu(p.head % 2)
                if p.head is not None and p.i == 2:
                    head_sd()
                if p.tail is not None and p.i == 4:
                    tail_hi(p.tail)
                    tail_settle()

            def step(c, p, more):
                fc = p.fc
                grp, tail, head = (p.grp, p.tail, p.head) if more else (None, None, None)
                last = p.layer == 1 and p.n == FEATS - 1
                if head is not None and p.i == 0:
                    head_load((c + 1) * TPC + head)
                if p.layer == 0 and p.n == 0:
                    r_hi(R14_SLOT, FEATS - 1)
                unit(0, False)
                if fc and 1 < p.n <= TPC:
                    fc_gelu1(p.n - 1)
                if more and p.open is not None:
                    exps(p.open[1])
                if p.layer and p.n == 0:
                    x_hi(0, FEATS - 1)
                if tail is not None and p.i == 2:
                    tail_gate()
                if tail is not None and p.i == 4:
                    tail_store(c + 1, tail)
                if grp is not None:
                    copy_eT()
                unit(1, last)
                if more and p.open is not None:
                    weigh(p.open[1])
                if head is not None and p.i == 3:
                    head_gelu(head % 2)
                if fc and p.n == 1:
                    fc_gelu1(0)
                if fc and p.n == 5:
                    fc_gelu2(0)
                if more and p.follows is not None:
                    copy_eT()
                if fc and p.n == 5:
                    fc_gelu2(1)
                unit(2, last)
                if fc and p.n in (0, 4):
                    fc_sd()
                if p.n:
                    x_hi(p.layer, p.n - 1)
                if tail is not None and p.i == 2:
                    tail_copy()
                if head is not None and p.i == 2:
                    head_sd()
                if tail is not None and p.i == 4:
                    tail_settle()

            def plain_step(layer, n, pending, last=False):
                unit(0, False)
                if pending is not None:
                    x_hi(pending, n - 1 if pending == layer else FEATS - 1)
                unit(1, last)
                unit(2, last)

            def w1_stage(more):
                for k in range(FEATS):
                    ws, rs = w1_slots(k, more)
                    if k + 2 < FEATS:
                        w_hi(ws, (k + 2) % RING, H1)
                    elif more:
                        w_hi(ws, (k + 2) % RING)
                    if k == 0:
                        x_hi(1, FEATS - 1)
                    if more and k:
                        r_hi(rs, k - 1)

            def chunk(c, more):
                if more:
                    for p in plan:
                        step(c, p, True)
                else:
                    for p in plan[:FC_STEPS]:
                        step(c, p, False)
                    with act.Fori(FC_STEPS, FEATS) as n:
                        plain_step(0, n, 0)
                    plain_step(1, 0, 0)
                    with act.Fori(1, FEATS - 1) as n:
                        plain_step(1, n, 1)
                    plain_step(1, FEATS - 1, 1, True)
                w1_stage(more)

            act.sem_inc(S_free, 2)
            act.sem_inc(tp_free, 1)
            act.sem_inc(eT_free, 2)
            head_load(0)
            act.wait_ge(consts_ok, 1).then_inc(consts_ok, -1)
            for p in plan[:5]:
                opening_step(p)
            for u in range(2):
                act.wait_ge(raw_landed[u], DMA).then_inc(raw_landed[u], -DMA)
                af(Wh[:, u, :], raw[:, u, :], ACT.Copy).then_inc(hi_done, 1)
            for p in plan[5:]:
                opening_step(p)
            act.wait_ge(eT_free, 2).then_inc(eT_free, -1)
            for k in range(DIRECT, FEATS - 1):
                r_hi((2 + k - DIRECT) % RING, k, False)
            with act.Fori(0, nchunks - 1) as c:
                chunk(c, True)
            chunk(nchunks - 1, False)
            fc_sd()
            for j in range(TPC):
                fc_gelu1(j, j)
            fc_sd()
            fc_gelu2(0, 0)
            fc_gelu2(1, 1)
            act.wait_ge(logits_ready, 1).then_inc(logits_ready, -1)
            af(probs[:], logits[:, TPC:TPC + ntiles], ACT.Exp, scale=-1.0).then_inc(lexp_ready, 1)

        @block.vector
        def _(dve):
            v = nc.vector

            def done(ins):
                link(dve, dve_done, ins)

            def head_mask(par, t):
                done(v.tensor_scalar(keep[:, par, :], idx_all[:, t, 0:SEQ], 0.0, None, ALU.not_equal))
                done(v.tensor_scalar(mbias[:, par, :], idx_all[:, t, 0:SEQ], 0.0, MASKED, ALU.is_equal, ALU.mult))

            def head_var():
                dve.wait_ge(m_ready, 1).then_inc(m_ready, -1)
                done(v.tensor_tensor(xi[:], mps[:, 0:P], row("mm_b"), ALU.add))
                dve.sem_inc(bank4_free, 1)
                done(v.bn_stats(stats[:], xi[:]))
                v.bn_aggr(mv[:], stats[:]).then_inc(var_ready, 1)

            def head_norm():
                dve.wait_ge(sd_ready, 1).then_inc(sd_ready, -1)
                done(v.reciprocal(rstd[:], sd[:]))
                done(v.tensor_scalar(xi[:], xi[:], mv[:, 0:1], rstd[:], ALU.subtract, ALU.mult))
                done(v.tensor_tensor(xi[:], xi[:], row("mm_g"), ALU.mult))
                v.tensor_tensor(xi[:], xi[:], row("mm_lb"), ALU.add).then_inc(xi_ready, 1)

            def head_target(pair, par):
                dve.wait_ge(img_ready, 1).then_inc(img_ready, -1)
                dve.wait_ge(feat_landed[par], (pair + 1) * (3 * DMA))
                done(v.tensor_tensor(tgt[:], S[:, par, 2, :], S[:, par, 3, :], ALU.add))
                dve.sem_inc(tgt_ready, 1)

            def head_tT(par):
                dve.wait_ge(m_ready, 1).then_inc(m_ready, -1)
                done(v.tensor_copy(tT[:, par, :], mps[:, 0:P]))
                dve.sem_inc(tT_ready, 1)

            def head_T(par):
                dve.wait_ge(m_ready, 1).then_inc(m_ready, -1)
                done(v.tensor_tensor(Tt[:, par, :], mps[:, P:P + HID], row("ab1"), ALU.add))
                dve.sem_inc(bank4_free, 1)

            def times_target(par, at=0):
                dve.wait_ge(eT_ready, 1).then_inc(eT_ready, -1)
                v.tensor_tensor(teTs[at].rearrange("p (s b) -> p s b", s=SUB), eTs[at].rearrange("p (s b) -> p s b", s=SUB),
                                tT[:, par:par + 1, :].to_broadcast([P, SUB, P]), ALU.mult).then_inc(te_ready, 1)

            def hidden_sum(par, u):
                dve.wait_ge(h_ready, 1).then_inc(h_ready, -1)
                dve.sem_inc(eT_free, 1)
                v.tensor_tensor(hid[:], hps[:, u, 0:SUB * HID].rearrange("p (s h) -> p s h", s=SUB),
                                Tt[:, par:par + 1, :].to_broadcast([P, SUB, HID]), ALU.add).then_inc(hid_done, 1)

            def hidden_relu():
                dve.wait_ge(hid_done, 1).then_inc(hid_done, -1)
                v.scalar_tensor_tensor(out=hid[:], in0=hid[:], scalar=0.0,
                                       in1=row("aw2").rearrange("p (o h) -> p o h", o=1).to_broadcast([P, SUB, HID]),
                                       op0=ALU.max, op1=ALU.mult).then_inc(hid_done, 1)

            def scores(g, u):
                dve.wait_ge(hid_done, 1).then_inc(hid_done, -1)
                v.tensor_reduce(sc[:, g, u * SUB:(u + 1) * SUB], hid[:], AX.X, ALU.add).then_inc(hid_done, 1)

            def scores_end():
                dve.wait_ge(hid_done, 1).then_inc(hid_done, -1)

            def softmax_max(par, g):
                k = slice(g * GRP, (g + 1) * GRP)
                done(v.scalar_tensor_tensor(out=sc[:, g, :], in0=sc[:, g, :], scalar=row("ab2"), in1=keep[:, par, k],
                                            op0=ALU.add, op1=ALU.mult))
                done(v.tensor_tensor(sc[:, g, :], sc[:, g, :], mbias[:, par, k], ALU.add))
                done(v.tensor_reduce(gmax[:], sc[:, g, :], AX.X, ALU.max))
                before = nmax[:, g - 1:g] if g else -LEAST
                v.tensor_scalar(nmax[:, g:g + 1], gmax[:], -1.0, before, ALU.mult, ALU.min).then_inc(sc_ready, 1)

            def softmax_sum(g):
                dve.wait_ge(p_ready, 1).then_inc(p_ready, -1)
                if g == 0:
                    done(v.tensor_copy(rsum[:, 0:1], gsum[:, 0:1]))
                else:
                    done(v.scalar_tensor_tensor(out=rsum[:, g:g + 1], in0=rsum[:, g - 1:g], scalar=corr[:, g:g + 1],
                                                in1=gsum[:, g:g + 1], op0=ALU.mult, op1=ALU.add))
                if g == NG - 1:
                    done(v.reciprocal(rinv[:], rsum[:, g:g + 1]))

            def history_sum(g, b, n, out=None):
                at = g * GRP
                x, y = e[:, at:at + n, :], e[:, at + b:at + b + n, :]
                v.tensor_tensor(x if out is None else out, x, y, ALU.add).then_inc(hist_done, 1)

            def history_step():
                dve.wait_ge(hist_done, 1).then_inc(hist_done, -1)

            def history_end(par, g):
                history_step()
                if g:
                    done(v.scalar_tensor_tensor(out=acc[:, par, :], in0=acc[:, par, :], scalar=corr[:, g:g + 1],
                                                in1=e[:, g * GRP, :], op0=ALU.mult, op1=ALU.add))
                dve.sem_inc(e_free, 1)
                if g == NG - 1:
                    dve.sem_inc(acc_ready, 1)

            def tail_history(par):
                dve.wait_ge(acc_ready, 1).then_inc(acc_ready, -1)
                done(v.tensor_scalar(S[:, par, 4, :], acc[:, par, :], rinv[:], None, ALU.mult))
                done(v.tensor_reduce(z5[:], S[:, par, :, :], AX.X, ALU.add))

            def tail_gate_logits():
                w1v = row("se_w1").rearrange("p (j f) -> p j f", j=2)
                done(v.scalar_tensor_tensor(out=se10[:].rearrange("p (j f) -> p j f", j=2),
                                            in0=z5[:].rearrange("p (o f) -> p o f", o=1).to_broadcast([P, 2, FIELDS]),
                                            scalar=1.0 / EMB, in1=w1v, op0=ALU.mult, op1=ALU.mult))
                done(v.tensor_reduce(se2[:], se10[:].rearrange("p (j f) -> p j f", j=2), AX.X, ALU.add))
                done(v.tensor_tensor(se2[:], se2[:], row("se_b1"), ALU.add))
                done(v.tensor_scalar(se2[:], se2[:], 0.0, None, ALU.max))
                w2v = row("se_w2").rearrange("p (f j) -> p f j", j=2)
                done(v.tensor_tensor(se10[:].rearrange("p (f j) -> p f j", j=2),
                                     se2[:].rearrange("p (o j) -> p o j", o=1).to_broadcast([P, FIELDS, 2]), w2v, ALU.mult))
                done(v.tensor_reduce(g5[:], se10[:].rearrange("p (f j) -> p f j", j=2), AX.X, ALU.add))
                done(v.tensor_tensor(g5[:], g5[:], row("se_b2"), ALU.add))
                dve.sem_inc(gate_ready, 1)

            def tail_gate_apply(par):
                dve.wait_ge(gexp_ready, 1).then_inc(gexp_ready, -1)
                done(v.tensor_scalar(g5[:], g5[:], 1.0, None, ALU.add))
                done(v.reciprocal(g5[:], g5[:]))
                done(v.tensor_tensor(S[:, par, :, :], S[:, par, :, :],
                                     g5[:].rearrange("p (f o) -> p f o", o=1).to_broadcast([P, FIELDS, EMB]), ALU.mult))
                dve.sem_inc(se_ready, 1)

            def tail_pairs():
                dve.wait_ge(m_ready, 1).then_inc(m_ready, -1)
                at = FIELDS
                for i in range(4):
                    n = FIELDS - 1 - i
                    v.tensor_tensor(dn[:, at:at + n, :], dn[:, i + 1:FIELDS, :],
                                    mps[:, i * P:(i + 1) * P].rearrange("p (o b) -> p o b", o=1).to_broadcast([P, n, P]),
                                    ALU.mult).then_inc(dve_done, 1)
                    at += n
                dve.wait_ge(dve_done, 4).then_inc(dve_done, -4)
                dve.sem_inc(bank4_free, 1)
                dve.sem_inc(dn_full, 1)

            def tail_lo(j):
                dve.wait_ge(hi_done, 1).then_inc(hi_done, -1)
                hi = X0h[:, 0:DIRECT, j * P:(j + 1) * P].bitcast(F32)
                done(v.tensor_tensor(X0l[:, 0:DIRECT, j * P:(j + 1) * P], dn[:, 0:DIRECT, :], hi, ALU.subtract))

            def w_lo(raw_slot, slot, n=KG * P):
                dve.wait_ge(hi_done, 1).then_inc(hi_done, -1)
                v.tensor_tensor(Wl[:, slot, 0:n], raw[:, raw_slot, 0:n], Wh[:, slot, 0:n].bitcast(F32),
                                ALU.subtract).then_inc(lo_done, 1)

            def w_out():
                dve.wait_ge(lo_done, 1).then_inc(lo_done, -1)
                dve.sem_inc(w_ready, 1)
                dve.sem_inc(raw_free, 1)

            def r_lo(raw_slot, k):
                dve.wait_ge(hi_done, 1).then_inc(hi_done, -1)
                done(v.tensor_tensor(X0l[:, k, :], raw[:, raw_slot, 0:NB], X0h[:, k, :].bitcast(F32), ALU.subtract))
                dve.sem_inc(x_ready, 1)
                dve.sem_inc(raw_free, 1)

            def x_sum(layer, n):
                v.tensor_tensor(xnew[:], X0h[:, n, :].bitcast(F32), X0l[:, n, :].bitcast(F32), ALU.add).then_inc(sum_done, 1)
                if layer == 1:
                    v.tensor_tensor(xsum[:], X1h[:, n, :].bitcast(F32), X1l[:, n, :].bitcast(F32),
                                    ALU.add).then_inc(sum_done, 1)

            def x_scale(layer, n):
                dve.wait_ge(sum_done, 1 + layer).then_inc(sum_done, -1 - layer)
                dve.wait_ge(mm_done, 1).then_inc(mm_done, -1)
                a, _ = COLS["cb"]
                bias = cols[:, bass.ds(n + (a + layer * FEATS), 1)]
                v.scalar_tensor_tensor(out=xnew[:], in0=xps[:, n % BANKS, :], scalar=bias, in1=xnew[:],
                                       op0=ALU.add, op1=ALU.mult).then_inc(scaled, 1)

            def x_end(layer):
                dve.wait_ge(scaled, 1).then_inc(scaled, -1)
                dve.sem_inc(bank_free, 1)
                if layer == 1:
                    done(v.tensor_tensor(xnew[:], xnew[:], xsum[:], ALU.add))
                dve.sem_inc(xnew_ready, 1)

            def x_new(layer, n):
                x_sum(layer, n)
                x_scale(layer, n)
                x_end(layer)

            def x_lo(layer, n):
                Xh, Xl = (X1h, X1l) if layer == 0 else (X0h, X0l)
                dve.wait_ge(xhi_done, 1).then_inc(xhi_done, -1)
                done(v.tensor_tensor(Xl[:, n, :], xnew[:], Xh[:, n, :].bitcast(F32), ALU.subtract))
                dve.sem_inc(x_ready, 1)

            def unit(q, last_layer):
                w_lo(w_slot(q), (q + 2) % RING, H1 if last_layer and q > 0 else KG * P)

            def fc_stats(j, x):
                done(v.bn_stats(fstats[:], x))
                done(v.bn_aggr(fmv[:, j, :], fstats[:]))

            def fc_rstd():
                dve.wait_ge(fsd_ready, 1).then_inc(fsd_ready, -1)
                done(v.reciprocal(frstd[:], fsd[:]))

            def fc_norm(j, x):
                return v.tensor_scalar(x, x, fmv[:, j, 0:1], frstd[:, j:j + 1], ALU.subtract, ALU.mult)

            def fc_bias2(j, bank=FCB):
                dve.wait_ge(fmm_ready, 1).then_inc(fmm_ready, -1)
                done(v.tensor_tensor(h2(j), xps[:, bank, 0:H2], row("b2"), ALU.add))
                if bank == FCB:
                    dve.sem_inc(bank4_free, 1)

            def fc_between(j):
                fc_bias2(j - 1)
                if j < TPC:
                    fc_norm(j, h1[:, j, :]).then_inc(h1n_ready, 1)
                fc_stats(j - 1, h2(j - 1))

            def fc_norms2():
                fc_rstd()
                for j in range(0, TPC, 2):
                    done(fc_norm(j, h2(j)))
                    fc_norm(j + 1, h2(j + 1)).then_inc(h2n_ready, 1)

            def fc_logits(c):
                dve.wait_ge(fmm_ready, 1).then_inc(fmm_ready, -1)
                done(v.tensor_scalar(logits[:, bass.ds(c * TPC, TPC)], mps[:, 0:TPC], row("b3"), None, ALU.add))
                dve.sem_inc(bank4_free, 1)

            def opening_step(p):
                if p.head is not None and p.i == 4:
                    head_target(p.head // 2, p.head % 2)
                if p.open is not None:
                    softmax_max(p.open[0] % 2, p.open[1])
                if p.tail is not None and p.i == 2:
                    tail_gate_logits()
                if p.grp is not None:
                    times_target(p.grp % 2, 1)
                if p.head_before is not None:
                    head_T(p.head_before % 2)
                if p.head is not None and p.i == 3:
                    head_norm()
                if p.grp is not None:
                    hidden_sum(p.grp % 2, 0)
                    hidden_relu()
                    scores(p.g, 0)
                    scores_end()
                if p.tail is not None and p.i == 1:
                    tail_history(p.tail % 2)
                if p.tail is not None and p.i == 2:
                    tail_gate_apply(p.tail % 2)
                if p.head is not None and p.i == 1:
                    head_mask(p.head % 2, p.head)
                if p.head is not None and p.i == 2:
                    head_var()
                if p.head is not None and p.i == 4:
                    head_tT(p.head % 2)
                if p.tail is not None and p.i == 3:
                    tail_pairs()
                if p.follows is not None:
                    times_target(p.follows[0] % 2)
                if p.open is not None:
                    opened, g = p.open
                    softmax_sum(g)
                    dve.wait_ge(weighed, 1).then_inc(weighed, -1)
                    history_sum(g, 5, 5)
                if p.grp is not None:
                    hidden_sum(p.grp % 2, 1)
                if p.open is not None:
                    history_step()
                    history_sum(g, 2, 2)
                if p.grp is not None:
                    hidden_relu()
                if p.open is not None:
                    history_step()
                    history_sum(g, 1, 1)
                if p.grp is not None:
                    scores(p.g, 1)
                if p.open is not None:
                    history_step()
                    history_sum(g, 4, 1, acc[:, opened % 2:opened % 2 + 1, :] if g == 0 else None)
                if p.grp is not None:
                    scores_end()
                if p.open is not None:
                    history_end(opened % 2, g)
                if p.tail is not None and p.i == 4:
                    tail_lo(p.tail)

            def step(c, p, more):
                fc = p.fc
                grp, tail, head = (p.grp, p.tail, p.head) if more else (None, None, None)
                prev = (p.layer, p.n - 1) if p.n else (0, FEATS - 1) if p.layer else None
                last = p.layer == 1 and p.n == FEATS - 1
                if more and p.open is not None:
                    softmax_max(p.open[0] % 2, p.open[1])
                if p.layer == 0 and p.n == 0:
                    r_lo(R14_SLOT, FEATS - 1)
                unit(0, False)
                if prev is not None:
                    x_sum(*prev)
                w_out()
                if p.n == 0 and p.layer:
                    x_scale(*prev)
                    x_end(0)
                if fc and p.n == 0:
                    dve.wait_ge(mm_done, 1).then_inc(mm_done, -1)
                    for b in range(1, TPC):
                        h1_bias(b)
                    fc_stats(0, h1[:, 0, :])
                    fc_stats(1, h1[:, 1, :])
                if p.head_before is not None and more:
                    head_T(p.head_before % 2)
                if fc and p.n == 5:
                    fc_norms2()
                if tail is not None and p.i == 2:
                    tail_gate_logits()
                if head is not None and p.i == 3:
                    head_norm()
                if head is not None and p.i == 4:
                    head_target((c + 1) * (TPC // 2) + head // 2, head % 2)
                if grp is not None:
                    hidden_sum(grp % 2, 0)
                if p.n:
                    x_scale(*prev)
                if grp is not None:
                    times_target(grp % 2)
                    hidden_relu()
                unit(1, last)
                if grp is not None:
                    scores(p.g, 0)
                w_out()
                if p.n:
                    x_end(p.layer)
                if grp is not None:
                    scores_end()
                if p.layer and p.n == 0:
                    x_lo(*prev)
                if fc and p.n == 0:
                    fc_stats(2, h1[:, 2, :])
                    fc_stats(3, h1[:, 3, :])
                    dve.sem_inc(fvar_ready, 1)
                if fc and 1 < p.n <= TPC:
                    fc_between(p.n)
                if fc and p.n == TPC:
                    dve.sem_inc(fvar_ready, 1)
                if head is not None and p.i == 2:
                    head_var()
                if tail is not None and p.i == 2:
                    tail_gate_apply(tail % 2)
                if grp is not None:
                    hidden_sum(grp % 2, 1)
                if head is not None and p.i == 4:
                    head_tT(head % 2)
                if grp is not None:
                    hidden_relu()
                if more and p.follows is not None:
                    times_target(p.follows[0] % 2)
                if grp is not None:
                    scores(p.g, 1)
                unit(2, last)
                w_out()
                if grp is not None:
                    scores_end()
                if p.n:
                    x_lo(*prev)
                if fc and p.n == 0:
                    fc_rstd()
                    fc_norm(0, h1[:, 0, :]).then_inc(h1n_ready, 1)
                if fc and p.n == 1:
                    fc_between(1)
                if fc and p.n == 5:
                    fc_logits(c)
                if more and p.open is not None:
                    softmax_sum(p.open[1])
                if tail is not None and p.i == 1:
                    tail_history(tail % 2)
                if tail is not None and p.i == 3:
                    tail_pairs()
                if head is not None and p.i == 3:
                    head_mask(head % 2, (c + 1) * TPC + head)

            def plain_step(layer, n, pending, last=False):
                m = n - 1 if pending == layer else FEATS - 1
                unit(0, False)
                w_out()
                x_new(pending, m)
                unit(1, last)
                w_out()
                x_lo(pending, m)
                unit(2, last)
                w_out()

            def h1_bias(b):
                done(v.tensor_tensor(h1[:, b, :], xps[:, b, :], row("b1"), ALU.add))
                dve.sem_inc(bank_free if b < BANKS else bank4_free, 1)

            def w1_stage(more):
                for k in range(FEATS):
                    ws, rs = w1_slots(k, more)
                    if k == 0:
                        x_new(1, FEATS - 1)
                    if k == FEATS - 1:
                        dve.wait_ge(mm_done, 1).then_inc(mm_done, -1)
                        h1_bias(0)
                    if k + 2 < FEATS:
                        w_lo(ws, (k + 2) % RING, H1)
                    elif more:
                        w_lo(ws, (k + 2) % RING)
                    if k + 2 < FEATS or more:
                        w_out()
                    if k == 0:
                        x_lo(1, FEATS - 1)
                    if more and k:
                        r_lo(rs, k - 1)

            def chunk(c, more):
                if more:
                    for p in plan:
                        step(c, p, True)
                else:
                    for p in plan[:FC_STEPS]:
                        step(c, p, False)
                    with dve.Fori(FC_STEPS, FEATS) as n:
                        plain_step(0, n, 0)
                    plain_step(1, 0, 0)
                    with dve.Fori(1, FEATS - 1) as n:
                        plain_step(1, n, 1)
                    plain_step(1, FEATS - 1, 1, True)
                w1_stage(more)

            dve.sem_inc(raw_free, RING)
            dve.sem_inc(bank_free, 1)
            dve.sem_inc(bank4_free, 1)
            done(v.memset(eps[:], EPS))
            dve.wait_ge(consts_in, NCONST * DMA)
            done(v.tensor_tensor(A02[:], aw1[:, 0, :], aw1[:, 2, :], ALU.add))
            done(v.tensor_copy(A3[:], aw1[:, 3, :]))
            done(v.tensor_tensor(A12[:], aw1[:, 1, :], aw1[:, 2, :], ALU.subtract))
            done(v.tensor_scalar(col("cb", 0, FEATS), col("cb", 0, FEATS), 1.0, None, ALU.add))
            dve.sem_inc(consts_ok, 2)
            dve.wait_ge(idx_in, DMA)
            for p in plan[:5]:
                opening_step(p)
            for u in range(2):
                w_lo(u, u)
                w_out()
            for p in plan[5:]:
                opening_step(p)
            dve.sem_inc(x_ready, DIRECT)
            for k in range(DIRECT, FEATS - 1):
                r_lo((2 + k - DIRECT) % RING, k)
            dve.wait_ge(bank4_free, 1).then_inc(bank4_free, -1)
            done(v.memset(xps[:, 1:TPC, :], 0.0))
            done(v.memset(h1[:, 0, :], 0.0))
            dve.sem_inc(mm_done, 1)
            with dve.Fori(0, nchunks - 1) as c:
                chunk(c, True)
            chunk(nchunks - 1, False)
            fc_stats(0, h1[:, 0, :])
            dve.wait_ge(mm_done, 1).then_inc(mm_done, -1)
            for j in range(1, TPC):
                h1_bias(j)
                fc_stats(j, h1[:, j, :])
            dve.sem_inc(fvar_ready, 1)
            fc_rstd()
            for j in range(TPC):
                fc_norm(j, h1[:, j, :]).then_inc(h1n_ready, 1)
            for j in range(TPC):
                fc_bias2(j, j)
                fc_stats(j, h2(j))
            dve.sem_inc(fvar_ready, 1)
            fc_norms2()
            fc_logits(nchunks)
            dve.sem_inc(logits_ready, 1)
            dve.wait_ge(lexp_ready, 1).then_inc(lexp_ready, -1)
            done(v.tensor_scalar(probs[:], probs[:], 1.0, None, ALU.add))
            done(v.reciprocal(probs[:], probs[:]))
            dve.sem_inc(probs_ready, 1)
            dve.wait_ge(probsT_ready, 1).then_inc(probsT_ready, -1)
            done(v.tensor_copy(xi[0:ntiles, :], xps[0:ntiles, FCB, 0:P]))
            dve.sem_inc(res_ready, 1)


def kernel(**inputs):
    import numpy as np
    import concourse.bacc as bacc
    from concourse.bass_utils import run_bass_kernel_spmd as run

    x = {k.removeprefix("L0_rec_"): np.asarray(a) for k, a in inputs.items()}
    batch = x["r_item_seq"].shape[0]
    tiles = batch // P

    def column(name):
        return x[name].reshape(-1, 1)

    idx = np.concatenate([x["r_item_seq"], column("r_item_id"), column("r_likes_level"), column("r_views_level")], axis=1)
    rows = {"mm_b": x["mm_b"], "mm_g": x["mm_ln_g"], "mm_lb": x["mm_ln_b"], "ab1": x["ab1"], "aw2": x["aw2"], "b1": x["b1"],
            "b2": x["b2"], "se_w1": x["se_w1"].T, "se_b1": x["se_b1"], "se_w2": x["se_w2"].T, "se_b2": x["se_b2"],
            "ab2": x["ab2"], "b3": x["b3"]}
    cols = {"g1": x["ln1g"], "lb1": x["ln1b"], "g2": x["ln2g"], "lb2": x["ln2b"], "w3": x["w3"], "cb": x["cross_bias"]}
    host = {
        "idx": idx.reshape(tiles, P, SEQ + 3).transpose(1, 0, 2),
        "item_table": x["item_table"],
        "cate_table": x["cate_table"],
        "embT": x["r_item_emb_d128"].T,
        "rows": np.broadcast_to(np.concatenate([rows[k].reshape(-1) for k in ROWS]), (P, NROWS)),
        "cols": np.concatenate([cols[k].reshape(-1, P).T for k in COLS], axis=1),
        "mm_w": x["mm_w"],
        "aw1": x["aw1"],
        "bil_W": x["bil_W"],
        "cross_K": x["cross_K"].reshape(2, UNITS, KG, P, FEATS, P).transpose(0, 4, 1, 3, 2, 5)
                   .reshape(2 * FEATS * UNITS, P, KG * P),
        "w1": x["w1"],
        "w2": x["w2"],
    }
    nc = bacc.Bacc("TRN2", target_bir_lowering=False, num_devices=1, dynamic_dma_scratch_size=8192)
    arrays, args = {}, []
    for name, a in host.items():
        a = np.ascontiguousarray(a)
        arrays[f"in_{name}"] = a
        args.append(nc.dram_tensor(f"in_{name}", a.shape, mybir.dt.from_np(a.dtype), kind="ExternalInput").ap())
    out = nc.dram_tensor("out_probs", (tiles, P), F32, kind="ExternalOutput").ap()
    build(nc, *args, out, tiles)
    r = run(nc, [arrays], core_ids=[0])
    return r.results[0]["out_probs"].reshape(batch)
```
